# Optimizing a Trainium2 kernel written in Bass

```python
import numpy as np
import jax
import jax.numpy as jnp

def _softmax(x, axis=-1):
    return jax.nn.softmax(x, axis=axis)

def _gelu(x):
    return jax.nn.gelu(x, approximate=True)

def _silu(x):
    return jax.nn.silu(x)

def _sigmoid(x):
    return jax.nn.sigmoid(x)

def _layernorm(x, axis=-1, eps=1e-05):
    m = jnp.mean(x, axis=axis, keepdims=True)
    v = jnp.var(x, axis=axis, keepdims=True)
    return (x - m) / jnp.sqrt(v + eps)

def _scatter_add(tgt, idx, src, axis=0):
    return tgt.at[idx].add(src)

def _segment_sum(src, seg, n):
    return jax.ops.segment_sum(src, seg, n)
kernel_name = 'mk_xattn_ffn_d2_seqx_r8_610894'

def setup_inputs(seed: int=0):
    np.random.seed(seed)
    _w = jnp.asarray

    def _rec_inputs():
        import jax
        import jax.numpy as jnp
        _rk = jax.random.key(seed)
        x = 7.22e-05 + 1 * jax.random.normal(jax.random.fold_in(_rk, 1), (32, 128, 128), jnp.float32)
        _lenS = 128 - jax.random.randint(jax.random.fold_in(_rk, 7), (32,), 0, max(1, 128 // 4) + 1, jnp.int32)
        _lenS2 = 128 - jax.random.randint(jax.random.fold_in(_rk, 8), (32,), 0, max(1, 128 // 4) + 1, jnp.int32)
        _ctx_1024P = jax.random.normal(jax.random.fold_in(_rk, 11), (32, 16, 128), jnp.float32)
        _ctx_1024c = jax.random.dirichlet(jax.random.fold_in(_rk, 511), 0.3 * jnp.ones((16,), jnp.float32), (32, 128))
        _ctx_1024t = jnp.einsum('bsk,bkd->bsd', _ctx_1024c, _ctx_1024P)
        _ctx_1024t = _ctx_1024t * jax.lax.rsqrt(jnp.mean(jnp.square(_ctx_1024t)) + 1e-12) * 0.953939
        ctx_1024 = 4.13588e-05 + 0.999923 * (_ctx_1024t + 0.3 * jax.random.normal(jax.random.fold_in(_rk, 611), (32, 128, 128), jnp.float32))
        return (x, ctx_1024)
    x, ctx_1024 = _rec_inputs()

    def _L0_xattn_setup():
        import jax, jax.numpy as jnp
        import numpy as np
        import math
        EMB = 128
        HEADS = 16
        HEAD_DIM = EMB // HEADS
        key = jax.random.key(seed)
        ks = jax.random.split(key, 11)
        B, S = (4, 256)
        s = 1.0 / math.sqrt(EMB)
        return {'query': jax.random.normal(ks[0], (B, S, EMB), jnp.float32), 'key': jax.random.normal(ks[1], (B, S, EMB), jnp.float32), 'value': jax.random.normal(ks[2], (B, S, EMB), jnp.float32), 'Wq': jax.random.normal(ks[3], (EMB, EMB), jnp.float32) * s, 'bq': jax.random.normal(ks[4], (EMB,), jnp.float32) * s, 'Wk': jax.random.normal(ks[5], (EMB, EMB), jnp.float32) * s, 'bk': jax.random.normal(ks[6], (EMB,), jnp.float32) * s, 'Wv': jax.random.normal(ks[7], (EMB, EMB), jnp.float32) * s, 'bv': jax.random.normal(ks[8], (EMB,), jnp.float32) * s, 'Wo': jax.random.normal(ks[9], (EMB, EMB), jnp.float32) * s, 'bo': jax.random.normal(ks[10], (EMB,), jnp.float32) * s}
    _L0_xattn_all = _L0_xattn_setup()
    _L0_xattn_in = {k: v for k, v in _L0_xattn_all.items() if k in ('Wq', 'bq', 'Wk', 'bk', 'Wv', 'bv', 'Wo', 'bo')}
    del _L0_xattn_all

    def _L0_ffn_setup():
        import jax, jax.numpy as jnp
        import numpy as np
        from jax import lax
        B, S, D = (4, 256, 128)
        E = 8
        K = 2
        F = 408
        NORM_TOPK = True
        key = jax.random.key(seed)
        ks = jax.random.split(key, 8)
        sd = 0.02
        return {'x': jax.random.normal(ks[0], (B, S, D), jnp.float32), 'gate_w': jax.random.normal(ks[1], (E, D), jnp.float32) * sd, 'gate_b': jnp.zeros((E,), jnp.float32), 'up_w': jax.random.normal(ks[2], (E, F, D), jnp.float32) * sd, 'up_b': jnp.zeros((E, F), jnp.float32), 'gp_w': jax.random.normal(ks[3], (E, F, D), jnp.float32) * sd, 'gp_b': jnp.zeros((E, F), jnp.float32), 'down_w': jax.random.normal(ks[4], (E, D, F), jnp.float32) * sd, 'down_b': jnp.zeros((E, D), jnp.float32)}
    _L0_ffn_all = _L0_ffn_setup()
    _L0_ffn_in = {k: v for k, v in _L0_ffn_all.items() if k in ('gate_w', 'gate_b', 'up_w', 'up_b', 'gp_w', 'gp_b', 'down_w', 'down_b')}
    del _L0_ffn_all

    def _L1_xattn_setup():
        import jax, jax.numpy as jnp
        import numpy as np
        D_MODEL = 128
        N_HEADS = 16
        D_KEYS = D_MODEL // N_HEADS
        key = jax.random.key(seed)
        ks = jax.random.split(key, 11)
        B, L, S = (2, 256, 256)
        inp = {'queries': jax.random.normal(ks[0], (B, L, D_MODEL), dtype=jnp.float32), 'keys': jax.random.normal(ks[1], (B, S, D_MODEL), dtype=jnp.float32), 'values': jax.random.normal(ks[2], (B, S, D_MODEL), dtype=jnp.float32), 'Wq': jax.random.normal(ks[3], (D_MODEL, D_MODEL), dtype=jnp.float32) / np.sqrt(D_MODEL), 'bq': jax.random.normal(ks[4], (D_MODEL,), dtype=jnp.float32) / np.sqrt(D_MODEL), 'Wk': jax.random.normal(ks[5], (D_MODEL, D_MODEL), dtype=jnp.float32) / np.sqrt(D_MODEL), 'bk': jax.random.normal(ks[6], (D_MODEL,), dtype=jnp.float32) / np.sqrt(D_MODEL), 'Wv': jax.random.normal(ks[7], (D_MODEL, D_MODEL), dtype=jnp.float32) / np.sqrt(D_MODEL), 'bv': jax.random.normal(ks[8], (D_MODEL,), dtype=jnp.float32) / np.sqrt(D_MODEL), 'Wo': jax.random.normal(ks[9], (D_MODEL, D_MODEL), dtype=jnp.float32) / np.sqrt(D_MODEL), 'bo': jax.random.normal(ks[10], (D_MODEL,), dtype=jnp.float32) / np.sqrt(D_MODEL)}
        return inp
    _L1_xattn_all = _L1_xattn_setup()
    _L1_xattn_in = {k: v for k, v in _L1_xattn_all.items() if k in ('Wq', 'bq', 'Wk', 'bk', 'Wv', 'bv', 'Wo', 'bo')}
    del _L1_xattn_all

    def _L1_ffn_setup():
        import jax, jax.numpy as jnp
        import numpy as np
        TOP_K = 2
        key = jax.random.key(seed)
        k0, k1, k2, k3, k4 = jax.random.split(key, 5)
        B, S, H, I, E = (1, 512, 128, 256, 8)
        hidden_states = jax.random.normal(k0, (B, S, H), dtype=jnp.float32)
        wg = jax.random.normal(k1, (E, H), dtype=jnp.float32) * 0.02
        w1 = jax.random.normal(k2, (E, I, H), dtype=jnp.float32) * 0.02
        w3 = jax.random.normal(k3, (E, I, H), dtype=jnp.float32) * 0.02
        w2 = jax.random.normal(k4, (E, H, I), dtype=jnp.float32) * 0.02
        return {'hidden_states': hidden_states, 'wg': wg, 'w1': w1, 'w3': w3, 'w2': w2}
    _L1_ffn_all = _L1_ffn_setup()
    _L1_ffn_in = {k: v for k, v in _L1_ffn_all.items() if k in ('wg', 'w1', 'w3', 'w2')}
    del _L1_ffn_all
    return {'x': x, 'ctx_1024': ctx_1024, 'L0_xattn_Wq': _L0_xattn_in['Wq'], 'L0_xattn_bq': _L0_xattn_in['bq'], 'L0_xattn_Wk': _L0_xattn_in['Wk'], 'L0_xattn_bk': _L0_xattn_in['bk'], 'L0_xattn_Wv': _L0_xattn_in['Wv'], 'L0_xattn_bv': _L0_xattn_in['bv'], 'L0_xattn_Wo': _L0_xattn_in['Wo'], 'L0_xattn_bo': _L0_xattn_in['bo'], 'L0_ffn_gate_w': _L0_ffn_in['gate_w'], 'L0_ffn_gate_b': _L0_ffn_in['gate_b'], 'L0_ffn_up_w': _L0_ffn_in['up_w'], 'L0_ffn_up_b': _L0_ffn_in['up_b'], 'L0_ffn_gp_w': _L0_ffn_in['gp_w'], 'L0_ffn_gp_b': _L0_ffn_in['gp_b'], 'L0_ffn_down_w': _L0_ffn_in['down_w'], 'L0_ffn_down_b': _L0_ffn_in['down_b'], 'L1_xattn_Wq': _L1_xattn_in['Wq'], 'L1_xattn_bq': _L1_xattn_in['bq'], 'L1_xattn_Wk': _L1_xattn_in['Wk'], 'L1_xattn_bk': _L1_xattn_in['bk'], 'L1_xattn_Wv': _L1_xattn_in['Wv'], 'L1_xattn_bv': _L1_xattn_in['bv'], 'L1_xattn_Wo': _L1_xattn_in['Wo'], 'L1_xattn_bo': _L1_xattn_in['bo'], 'L1_ffn_wg': _L1_ffn_in['wg'], 'L1_ffn_w1': _L1_ffn_in['w1'], 'L1_ffn_w3': _L1_ffn_in['w3'], 'L1_ffn_w2': _L1_ffn_in['w2']}

def reference(x, ctx_1024, L0_xattn_Wq, L0_xattn_bq, L0_xattn_Wk, L0_xattn_bk, L0_xattn_Wv, L0_xattn_bv, L0_xattn_Wo, L0_xattn_bo, L0_ffn_gate_w, L0_ffn_gate_b, L0_ffn_up_w, L0_ffn_up_b, L0_ffn_gp_w, L0_ffn_gp_b, L0_ffn_down_w, L0_ffn_down_b, L1_xattn_Wq, L1_xattn_bq, L1_xattn_Wk, L1_xattn_bk, L1_xattn_Wv, L1_xattn_bv, L1_xattn_Wo, L1_xattn_bo, L1_ffn_wg, L1_ffn_w1, L1_ffn_w3, L1_ffn_w2):
    import jax
    import jax.numpy as jnp

    def _L0_xattn_ref(query, key, value, Wq, bq, Wk, bk, Wv, bv, Wo, bo):
        import jax, jax.numpy as jnp
        import numpy as np
        import math
        EMB = 128
        HEADS = 16
        HEAD_DIM = EMB // HEADS
        B, S, _ = query.shape
        q = query @ Wq.T + bq
        k = key @ Wk.T + bk
        v = value @ Wv.T + bv
        q = q.reshape(B, S, HEADS, HEAD_DIM).transpose(0, 2, 1, 3)
        k = k.reshape(B, S, HEADS, HEAD_DIM).transpose(0, 2, 1, 3)
        v = v.reshape(B, S, HEADS, HEAD_DIM).transpose(0, 2, 1, 3)
        scale = 1.0 / math.sqrt(EMB)
        scores = jnp.einsum('bhqd,bhkd->bhqk', q, k) * scale
        probs = jax.nn.softmax(scores, axis=-1)
        out = jnp.einsum('bhqk,bhkd->bhqd', probs, v)
        out = out.transpose(0, 2, 1, 3).reshape(B, S, EMB)
        return out @ Wo.T + bo

    def _L0_ffn_ref(x, gate_w, gate_b, up_w, up_b, gp_w, gp_b, down_w, down_b):
        import jax, jax.numpy as jnp
        import numpy as np
        from jax import lax
        B, S, D = (4, 256, 128)
        E = 8
        K = 2
        F = 408
        NORM_TOPK = True
        bs, slen, dim = x.shape
        xf = x.reshape(-1, dim)
        N = xf.shape[0]
        scores = jax.nn.softmax(xf @ gate_w.T + gate_b, axis=-1)
        top_w, top_idx = lax.top_k(scores, K)
        if NORM_TOPK:
            top_w = top_w / (top_w.sum(-1, keepdims=True) + 1e-20)
        comb = jnp.zeros((N, E), xf.dtype).at[jnp.arange(N)[:, None], top_idx].add(top_w)

        def step(acc, p):
            uw, ub, gw, gb, dw, db, w = p
            h = jax.nn.silu((xf @ gw.T + gb) * (xf @ uw.T + ub))
            return (acc + w[:, None] * (h @ dw.T + db), None)
        y0 = jnp.zeros_like(xf)
        y, _ = lax.scan(step, y0, (up_w, up_b, gp_w, gp_b, down_w, down_b, comb.T))
        return y.reshape(bs, slen, dim)

    def _L1_xattn_ref(queries, keys, values, Wq, bq, Wk, bk, Wv, bv, Wo, bo):
        import jax, jax.numpy as jnp
        import numpy as np
        D_MODEL = 128
        N_HEADS = 16
        D_KEYS = D_MODEL // N_HEADS
        B, L, _ = queries.shape
        S = keys.shape[1]
        H, E = (N_HEADS, D_KEYS)
        scale = E ** (-0.5)
        q = (queries @ Wq.T + bq).reshape(B, L, H, E)
        k = (keys @ Wk.T + bk).reshape(B, S, H, E)
        v = (values @ Wv.T + bv).reshape(B, S, H, E)
        scores = jnp.einsum('blhe,bshe->bhls', q, k)
        attn = jax.nn.softmax(scores * scale, axis=-1)
        out = jnp.einsum('bhls,bshe->blhe', attn, v).reshape(B, L, H * E)
        return out @ Wo.T + bo

    def _L1_ffn_ref(hidden_states, wg, w1, w3, w2):
        import jax, jax.numpy as jnp
        import numpy as np
        TOP_K = 2
        orig_shape = hidden_states.shape
        H = orig_shape[-1]
        E = wg.shape[0]
        x = hidden_states.reshape(-1, H)
        router_logits = x @ wg.T
        probs = jax.nn.softmax(router_logits, axis=-1)
        topk_w, topk_idx = jax.lax.top_k(probs, TOP_K)
        topk_w = topk_w / jnp.sum(topk_w, axis=-1, keepdims=True)
        expert_w = jnp.sum(jax.nn.one_hot(topk_idx, E, dtype=x.dtype) * topk_w[..., None], axis=1)
        h1 = jnp.einsum('th,eih->tei', x, w1)
        h3 = jnp.einsum('th,eih->tei', x, w3)
        y = jnp.einsum('tei,ehi->teh', jax.nn.silu(h1) * h3, w2)
        out = jnp.einsum('te,teh->th', expert_w, y)
        return out.reshape(orig_shape)
    x = x + _L0_xattn_ref(_layernorm(x, axis=-1), ctx_1024, ctx_1024, L0_xattn_Wq, L0_xattn_bq, L0_xattn_Wk, L0_xattn_bk, L0_xattn_Wv, L0_xattn_bv, L0_xattn_Wo, L0_xattn_bo)
    x = x + _L0_ffn_ref(_layernorm(x, axis=-1), L0_ffn_gate_w, L0_ffn_gate_b, L0_ffn_up_w, L0_ffn_up_b, L0_ffn_gp_w, L0_ffn_gp_b, L0_ffn_down_w, L0_ffn_down_b)
    x = x + _L1_xattn_ref(_layernorm(x, axis=-1), ctx_1024, ctx_1024, L1_xattn_Wq, L1_xattn_bq, L1_xattn_Wk, L1_xattn_bk, L1_xattn_Wv, L1_xattn_bv, L1_xattn_Wo, L1_xattn_bo)
    x = x + _L1_ffn_ref(_layernorm(x, axis=-1), L1_ffn_wg, L1_ffn_w1, L1_ffn_w3, L1_ffn_w2)
    return x

_drawn_inputs = setup_inputs


def setup_inputs(seed=0):
    import zlib

    import numpy as np

    out = dict(_drawn_inputs(seed))
    spreads = {'L0_ffn_gate_b': (0.0, 0.1),
     'L0_ffn_up_b': (0.0, 0.8),
     'L0_ffn_gp_b': (0.0, 0.8),
     'L0_ffn_down_b': (0.0, 0.1)}
    factors = {'L0_xattn_bq': 8.0,
     'L0_xattn_bk': 8.0,
     'L0_ffn_up_w': 8.0,
     'L0_ffn_gp_w': 8.0,
     'L0_ffn_down_w': 8.0,
     'L1_xattn_bq': 3.901,
     'L1_xattn_bk': 8.0,
     'L1_ffn_wg': 8.0,
     'L1_ffn_w1': 8.0,
     'L1_ffn_w3': 8.0,
     'L1_ffn_w2': 8.0}
    for name, (base, spread) in spreads.items():
        noise = np.random.default_rng([zlib.crc32(name.encode()), seed]).standard_normal(out[name].shape)
        drawn = base * np.exp(spread * noise) if base else spread * noise
        out[name] = jnp.asarray(drawn.astype(out[name].dtype))
    for name, factor in factors.items():
        out[name] = (out[name] * factor).astype(out[name].dtype)
    return out
```

```python
from contextlib import ExitStack

import concourse.bass as bass
from concourse import mybir

F32 = mybir.dt.float32
ALU = mybir.AluOpType
ACT = mybir.ActivationFunctionType
AX_X = mybir.AxisListType.X

P = 128
D = 128
HEADS = 16
HD = D // HEADS
QUADS = 4
GROUPS = HEADS // QUADS
SLOT = 32
EXPERTS = 8
EPS = 1e-5


def need(engine, semaphore, count):
    if not isinstance(count, int) or count > 0:
        engine.wait_ge(semaphore, count)


def build_program(nc, t):
    B = t["x"].shape[0]
    NCH = B // 4
    CH = 4 * P

    with ExitStack() as ctx:
        def sb(name, shape):
            return ctx.enter_context(nc.sbuf_tensor(name, shape, F32))

        banks = [ctx.enter_context(nc.psum_tensor(f"bank{i}", [P, 512], F32)) for i in range(8)]

        X = sb("X", [P, B, D])
        XT = sb("XT", [D, B, P])
        comb = sb("comb", [P, B, EXPERTS])
        ident = sb("ident", [P, P])
        mean = sb("mean", [P, B])
        rstd = sb("rstd", [P, B])
        minus_half = sb("minus_half", [P, B])

        QB = sb("QB", [P, 2, GROUPS, QUADS, P])
        KB = sb("KB", [P, 2, GROUPS, QUADS, P])

        def load_constants():
            with ExitStack() as sems:
                loaded = sems.enter_context(nc.semaphore("loaded_const"))
                zeroed = sems.enter_context(nc.semaphore("ident_zeroed"))
                with nc.Block() as block:
                    @block.sync
                    def _(sp):
                        sp.dma_start(X[:], t["x"].rearrange("b p d -> p b d")).then_inc(loaded, 16)
                        sp.wait_ge(loaded, 16)

                    @block.gpsimd
                    def _(pool):
                        nc.gpsimd.memset(QB[:], 0.0)
                        nc.gpsimd.memset(KB[:], 0.0)
                        nc.gpsimd.memset(minus_half[:], -0.5)
                        nc.gpsimd.memset(ident[:], 0.0).then_inc(zeroed, 1)
                        pool.wait_ge(zeroed, 1)
                        nc.gpsimd.affine_select(out=ident[:], in_=ident[:], compare_op=ALU.not_equal, fill=1.0,
                                                base=0, pattern=[[-1, P]], channel_multiplier=1)

        def layer_norm_stats(tag):
            with ExitStack() as inner:
                stats = inner.enter_context(nc.sbuf_tensor(f"stats_{tag}", [P, B, 6], F32))
                half = inner.enter_context(nc.sbuf_tensor(f"half_{tag}", [P, 3, B], F32))
                stats_done = inner.enter_context(nc.semaphore(f"stats_done_{tag}"))
                aggr_done = inner.enter_context(nc.semaphore(f"aggr_done_{tag}"))
                eps_done = inner.enter_context(nc.semaphore(f"eps_done_{tag}"))
                with nc.Block() as block:
                    @block.vector
                    def _(dve):
                        with dve.Fori(0, B) as b:
                            nc.vector.bn_stats(stats[:, b, :], X[:, b, :]).then_inc(stats_done, 1)
                        dve.wait_ge(stats_done, B)
                        V = nc.vector
                        mean_e, mean_o, sq_e, sq_o = (stats[:, :, k] for k in (1, 4, 2, 5))
                        V.tensor_tensor(half[:, 0, :], mean_e, mean_o, ALU.add).then_inc(aggr_done, 1)
                        V.tensor_tensor(half[:, 1, :], mean_e, mean_o, ALU.subtract).then_inc(aggr_done, 1)
                        V.tensor_tensor(half[:, 2, :], sq_e, sq_o, ALU.add).then_inc(aggr_done, 1)
                        dve.wait_ge(aggr_done, 3)
                        V.tensor_scalar(mean[:], half[:, 0, :], 0.5, None, ALU.mult).then_inc(aggr_done, 1)
                        V.scalar_tensor_tensor(half[:, 1, :], half[:, 1, :], 0.25, half[:, 1, :], ALU.mult,
                                               ALU.mult).then_inc(aggr_done, 1)
                        dve.wait_ge(aggr_done, 5)
                        V.scalar_tensor_tensor(rstd[:], half[:, 2, :], 1.0 / D, half[:, 1, :], ALU.mult,
                                               ALU.add).then_inc(aggr_done, 1)

                    @block.gpsimd
                    def _(pool):
                        pool.wait_ge(aggr_done, 6)
                        nc.gpsimd.tensor_scalar(rstd[:], rstd[:], 1.0, EPS, ALU.mult,
                                                ALU.add).then_inc(eps_done, 1)
                        pool.wait_ge(eps_done, 1)
                        nc.gpsimd.tensor_tensor(rstd[:], rstd[:], minus_half[:], ALU.pow)

        def attention(layer):
            tag = f"L{layer}"
            scale = (1.0 / D ** 0.5) if layer == 0 else HD ** -0.5
            with ExitStack() as inner:
                def isb(name, shape):
                    return inner.enter_context(nc.sbuf_tensor(f"{name}_{tag}", shape, F32))

                def sem(name):
                    return inner.enter_context(nc.semaphore(f"{name}_{tag}"))

                wq = isb("wq", [D, GROUPS, P])
                wk = isb("wk", [D, GROUPS, P])
                wv = isb("wv", [D, D])
                wo = isb("wo", [D, D])
                bq = isb("bq", [P, GROUPS])
                bk = isb("bk", [P, GROUPS])
                bv = isb("bv", [P, D])
                bo = isb("bo", [P, D])
                C = isb("C", [P, 2, D])
                XN = isb("XN", [P, 2, D])
                XB = isb("XB", [P, 2, D])
                XCT = isb("XCT", [D, 2, 2, P])
                QS = isb("QS", [P, 2, GROUPS, P])
                QA = isb("QA", [P, 2, GROUPS, P])
                KS = isb("KS", [P, 2, GROUPS, P])
                VA = isb("VA", [P, 2, HEADS, SLOT])
                NM = isb("NM", [P, 2, GROUPS, P])
                MX = isb("MX", [P, 2, HEADS])
                E = isb("E", [P, GROUPS, QUADS, P])
                OS = isb("OS", [P, 2, GROUPS, P])
                RD = isb("RD", [P, 2, HEADS])
                ON = isb("ON", [P, 2, D])
                ONT = isb("ONT", [D, 2, P])

                bank_t, bank_q, bank_k, bank_o = banks[0], banks[1], banks[2], banks[7]
                bank_s, bank_st = banks[3:5], banks[5:7]

                params_in = sem("params_in")
                ctx_in = [sem("ctx_in0"), sem("ctx_in1")]
                kb_in = [sem("kb_in0"), sem("kb_in1")]
                qb_in = [sem("qb_in0"), sem("qb_in1")]
                fill_done = sem("fill_done")
                xn_ready, xb_ready = sem("xn_ready"), sem("xb_ready")
                t_done, xct_ready = sem("t_done"), sem("xct_ready")
                q_done, k_done, v_done = sem("q_done"), sem("k_done"), sem("v_done")
                q_ready, k_ready, v_ready = sem("q_ready"), sem("k_ready"), sem("v_ready")
                s_done, max_done, nm_ready = sem("s_done"), sem("max_done"), sem("nm_ready")
                mt_done, qa_ready = sem("mt_done"), sem("qa_ready")
                st_done, exp_done, pv_done, os_ready = sem("st_done"), sem("exp_done"), sem("pv_done"), sem("os_ready")
                ot_done, rd_ready, on_ready = sem("ot_done"), sem("rd_ready"), sem("on_ready")
                ont_done, ont_ready = sem("ont_done"), sem("ont_ready")
                out_done, x_done = sem("out_done"), sem("x_done")

                def pipeline(engine, step):
                    for n in range(-1, 4):
                        step(n, n % 2, n <= B - 2, n >= 0, n >= 1, n >= 2)
                    with engine.Fori(0, (B - 6) // 2) as j:
                        for u in range(2):
                            step(2 * j + 4 + u, u, True, True, True, True)
                    for n in range(B - 2, B + 2):
                        step(n, n % 2, n <= B - 2, n < B, n <= B, True)

                def loads(n, p):
                    return (n - p) * 8 + 16

                with nc.Block() as block:
                    @block.sync
                    def _(sp):
                        for dst, src in ((wq, "WqP"), (wk, "WkP"), (wv, "WvT"), (wo, "WoT"),
                                         (bq, "bqP"), (bk, "bkP"), (bv, "bvB"), (bo, "boB")):
                            sp.dma_start(dst[:], t[f"L{layer}_{src}"]).then_inc(params_in, 16)
                        for n in range(2):
                            sp.dma_start(C[:, n, :], t["ctx"][n]).then_inc(ctx_in[n], 16)

                        def spread(dst, src, p, landed):
                            for i in range(QUADS):
                                rows = slice(SLOT * i, SLOT * i + SLOT)
                                sp.dma_start(dst[rows, p, :, i, :], src[rows, p, :, :]).then_inc(landed[p], 16)

                        def step(n, p, front, mid, back, tail):
                            q = 1 - p
                            if mid:
                                sp.wait_ge(qa_ready, n + 1)
                                spread(QB, QA, p, qb_in)
                            if front:
                                sp.wait_ge(k_ready, n + 2)
                                spread(KB, KS, q, kb_in)

                        def step_and_context(n, p, front, mid, back, tail):
                            step(n, p, front, mid, back, tail)
                            if not isinstance(n, int) or 0 <= n + 3 < B and n >= -1:
                                sp.wait_ge(t_done, n + 2)
                                sp.dma_start(C[:, 1 - p, :], context(n + 3)).then_inc(ctx_in[1 - p], 16)

                        def context(n):
                            return t["ctx"][n]

                        for n in range(-1, 4):
                            step_and_context(n, n % 2, True, n >= 0, n >= 1, n >= 2)
                        with sp.Fori(0, (B - 8) // 2) as j:
                            for u in range(2):
                                step_and_context(2 * j + 4 + u, u, True, True, True, True)
                        for n in range(B - 4, B):
                            step_and_context(n, n % 2, n <= B - 2, True, True, True)

                    @block.gpsimd
                    def _(pool):
                        nc.gpsimd.memset(VA[:], 0.0).then_inc(fill_done, 1)
                        nc.gpsimd.memset(NM[:], 0.0).then_inc(fill_done, 1)
                        pool.wait_ge(fill_done, 2)
                        nc.gpsimd.memset(VA[:, :, :, HD:HD + 1], 1.0).then_inc(fill_done, 1)
                        pool.wait_ge(params_in, 8 * 16)

                        def step(n, p, front, mid, back, tail):
                            if mid:
                                need(pool, x_done, n - 1)
                                nc.gpsimd.tensor_tensor(XB[:, p, :], X[:, n, :], bo[:], ALU.add).then_inc(xb_ready, 1)

                        pipeline(pool, step)

                    @block.tensor
                    def _(pe):
                        pe.wait_ge(params_in, 8 * 16)
                        pe.wait_ge(fill_done, 3)

                        def weigh(m, q, g):
                            pe.wait_ge(exp_done, 4 * m + g + 1)
                            if g == 0:
                                need(pe, os_ready, m)
                            for i in range(QUADS):
                                mm = nc.tensor.matmul(bank_o[SLOT * i:SLOT * i + SLOT, P * g:P * g + P],
                                                      VA[:, q, QUADS * g + i, :], E[:, g, i, :],
                                                      start=True, stop=True)
                            if g == GROUPS - 1:
                                mm.then_inc(pv_done, 1)

                        def step(n, p, front, mid, back, tail):
                            q = 1 - p
                            if mid:
                                pe.wait_ge(q_ready, n + 1)
                                pe.wait_ge(kb_in[p], 4 * loads(n, p))
                                for g in range(GROUPS):
                                    need(pe, max_done, 4 * n + g - 1)
                                    nc.tensor.matmul(bank_s[g % 2][:], QS[:, p, g, :], KB[:, p, g, :, :],
                                                     start=True, stop=True).then_inc(s_done, 1)
                            if front:
                                pe.wait_ge(xn_ready, n + 2)
                                pe.wait_ge(ctx_in[q], loads(n + 1, q))
                                need(pe, x_done, n - 2)
                                nc.tensor.transpose(bank_t[:, 0:P], XN[:, q, :], ident[:])
                                nc.tensor.transpose(bank_t[:, P:2 * P], C[:, q, :], ident[:]).then_inc(t_done, 1)
                            if tail:
                                pe.wait_ge(os_ready, n - 1)
                                need(pe, k_ready, n + 1) if mid else None
                                for g in range(GROUPS):
                                    mm = nc.tensor.transpose(bank_k[:, P * g:P * g + P], OS[:, p, g, :], ident[:])
                                mm.then_inc(ot_done, 1)
                            if mid:
                                pe.wait_ge(nm_ready, n + 1)
                                for g in range(GROUPS):
                                    mm = nc.tensor.matmul(bank_q[:, P * g:P * g + P], NM[:, p, g, :], ident[:],
                                                          start=True, stop=True)
                                mm.then_inc(mt_done, 1)
                            if back:
                                pe.wait_ge(v_ready, n)
                                pe.wait_ge(qb_in[q], 4 * loads(n - 1, q))
                                for g in range(GROUPS):
                                    need(pe, exp_done, 4 * (n - 1) + g - 1)
                                    nc.tensor.matmul(bank_st[g % 2][:], KS[:, q, g, :], QB[:, q, g, :, :],
                                                     start=True, stop=True).then_inc(st_done, 1)
                                    if g >= 1:
                                        weigh(n - 1, q, g - 1)
                                weigh(n - 1, q, GROUPS - 1)
                            if tail:
                                pe.wait_ge(on_ready, n - 1)
                                if front:
                                    pe.wait_ge(xct_ready, n + 2)
                                nc.tensor.transpose(bank_t[:, 0:P], ON[:, p, :], ident[:]).then_inc(ont_done, 1)
                            if front:
                                pe.wait_ge(xct_ready, n + 2)
                                for g in range(GROUPS):
                                    mm = nc.tensor.matmul(bank_k[:, P * g:P * g + P], wk[:, g, :], XCT[:, q, 1, :],
                                                          start=True, stop=True)
                                mm.then_inc(k_done, 1)
                                if tail:
                                    pe.wait_ge(ont_ready, n - 1)
                                nc.tensor.matmul(bank_t[:, 0:P], XCT[:, q, 1, :], wv[:],
                                                 start=True, stop=True).then_inc(v_done, 1)
                                if mid:
                                    pe.wait_ge(qa_ready, n + 1)
                                for g in range(GROUPS):
                                    mm = nc.tensor.matmul(bank_q[:, P * g:P * g + P], wq[:, g, :], XCT[:, q, 0, :],
                                                          start=True, stop=True)
                                mm.then_inc(q_done, 1)
                            if tail:
                                pe.wait_ge(ont_ready, n - 1)
                                if front:
                                    pe.wait_ge(v_ready, n + 2)
                                nc.tensor.matmul(bank_t[:, 0:P], ONT[:, p, :], wo[:],
                                                 start=True, stop=True).then_inc(out_done, 1)

                        pipeline(pe, step)

                    @block.scalar
                    def _(act):
                        def step(n, p, front, mid, back, tail):
                            q = 1 - p
                            if front:
                                act.wait_ge(t_done, n + 2)
                                need(act, q_done, n)
                                nc.scalar.activation(XCT[:, q, :, :], bank_t[:, 0:2 * P].rearrange("p (a b) -> p a b", a=2),
                                                     ACT.Copy).then_inc(xct_ready, 1)
                            if back:
                                for g in range(GROUPS):
                                    act.wait_ge(st_done, 4 * (n - 1) + g + 1)
                                    if g == 0:
                                        need(act, pv_done, n - 1)
                                    nc.scalar.activation(E[:, g, :, :], bank_st[g % 2][:].rearrange("p (i k) -> p i k", i=QUADS),
                                                         ACT.Exp, scale=scale).then_inc(exp_done, 1)
                                act.wait_ge(pv_done, n)
                                need(act, ot_done, n - 2)
                                nc.scalar.activation(OS[:, q, :, :], bank_o[:].rearrange("p (g k) -> p g k", g=GROUPS),
                                                     ACT.Copy).then_inc(os_ready, 1)
                            if tail:
                                act.wait_ge(ont_done, n - 1)
                                need(act, out_done, n - 3)
                                nc.scalar.activation(ONT[:, p, :], bank_t[:, 0:P], ACT.Copy).then_inc(ont_ready, 1)

                        pipeline(act, step)

                    @block.vector
                    def _(dve):
                        dve.wait_ge(params_in, 8 * 16)
                        dve.wait_ge(fill_done, 3)

                        def step(n, p, front, mid, back, tail):
                            q = 1 - p
                            if front:
                                need(dve, t_done, n)
                                nc.vector.tensor_scalar(XN[:, q, :], X[:, n + 1, :], mean[:, bass.ds(n + 1, 1)],
                                                        rstd[:, bass.ds(n + 1, 1)], ALU.subtract,
                                                        ALU.mult).then_inc(xn_ready, 1)
                            if mid:
                                for g in range(GROUPS):
                                    dve.wait_ge(s_done, 4 * n + g + 1)
                                    nc.vector.tensor_reduce(MX[:, p, QUADS * g:QUADS * g + QUADS],
                                                            bank_s[g % 2][:].rearrange("p (i k) -> p i k", i=QUADS),
                                                            AX_X, ALU.max).then_inc(max_done, 1)
                                dve.wait_ge(max_done, 4 * n + 4)
                                need(dve, mt_done, n - 1)
                                nc.vector.tensor_scalar(NM[:, p, :, HD:P:SLOT],
                                                        MX[:, p, :].rearrange("p (g i) -> p g i", g=GROUPS),
                                                        -1.0, None, ALU.mult).then_inc(nm_ready, 1)
                            if tail:
                                dve.wait_ge(ot_done, n - 1)
                                outs = bank_k[:].rearrange("p (h c) -> p h c", c=SLOT)
                                nc.vector.reciprocal(RD[:, p, :].rearrange("p (h o) -> p h o", o=1),
                                                     outs[:, :, HD:HD + 1]).then_inc(rd_ready, 1)
                                dve.wait_ge(rd_ready, n - 1)
                                need(dve, ont_done, n - 3)
                                nc.vector.tensor_tensor(ON[:, p, :].rearrange("p (h d) -> p h d", h=HEADS),
                                                        outs[:, :, 0:HD],
                                                        RD[:, p, :].unsqueeze(2).to_broadcast([P, HEADS, HD]),
                                                        ALU.mult).then_inc(on_ready, 1)
                            if mid:
                                dve.wait_ge(mt_done, n + 1)
                                if not isinstance(n, int) or n >= 2:
                                    dve.wait_ge(qb_in[p], 4 * loads(n - 2, p))
                                nc.vector.tensor_tensor(QA[:, p, :, :], bank_q[:].rearrange("p (g k) -> p g k", g=GROUPS),
                                                        QS[:, p, :, :], ALU.add).then_inc(qa_ready, 1)
                            if front:
                                dve.wait_ge(k_done, n + 2)
                                need(dve, pv_done, n)
                                if back:
                                    dve.wait_ge(kb_in[q], 4 * loads(n - 1, q))
                                nc.vector.tensor_tensor(KS[:, q, :, :], bank_k[:].rearrange("p (g k) -> p g k", g=GROUPS),
                                                        bk[:].unsqueeze(2).to_broadcast([P, GROUPS, P]),
                                                        ALU.add).then_inc(k_ready, 1)
                                dve.wait_ge(v_done, n + 2)
                                nc.vector.tensor_tensor(VA[:, q, :, 0:HD], bank_t[:, 0:P].rearrange("p (h d) -> p h d", h=HEADS),
                                                        bv[:].rearrange("p (h d) -> p h d", h=HEADS),
                                                        ALU.add).then_inc(v_ready, 1)
                                dve.wait_ge(q_done, n + 2)
                                need(dve, s_done, 4 * n)
                                need(dve, qa_ready, n)
                                nc.vector.tensor_tensor(QS[:, q, :, :], bank_q[:].rearrange("p (g k) -> p g k", g=GROUPS),
                                                        bq[:].unsqueeze(2).to_broadcast([P, GROUPS, P]),
                                                        ALU.add).then_inc(q_ready, 1)
                            if tail:
                                dve.wait_ge(out_done, n - 1)
                                dve.wait_ge(xb_ready, n - 1)
                                nc.vector.tensor_tensor(X[:, n - 2, :], bank_t[:, 0:P], XB[:, p, :],
                                                        ALU.add).then_inc(x_done, 1)

                        pipeline(dve, step)

        def route(layer):
            tag = f"R{layer}"
            with ExitStack() as inner:
                def isb(name, shape):
                    return inner.enter_context(nc.sbuf_tensor(f"{name}_{tag}", shape, F32))

                def sem(name):
                    return inner.enter_context(nc.semaphore(f"{name}_{tag}"))

                gate = isb("gate", [D, EXPERTS])
                gate_b = isb("gate_b", [P, EXPERTS])
                XN = isb("XN", [P, 2, 4, D])
                LG = isb("LG", [P, B, EXPERTS])
                PR = isb("PR", [P, B, EXPERTS])
                T1 = isb("T1", [P, B, EXPERTS])
                T2 = isb("T2", [P, B, EXPERTS])
                T3 = isb("T3", [P, B, EXPERTS])
                R1 = isb("R1", [P, B])
                V1 = isb("V1", [P, B])
                V2 = isb("V2", [P, B])
                KEEP = isb("KEEP", [P, B, EXPERTS])
                bank_t, bank_l = banks[0:2], banks[2]
                params_in = sem("params_in")
                xn_ready, t_done, xt_ready = sem("xn_ready"), sem("t_done"), sem("xt_ready")
                lg_done, chain, exp_in, exp_out = sem("lg_done"), sem("chain"), sem("exp_in"), sem("exp_out")
                keep_ready = sem("keep_ready")

                def chunks(engine, chunk):
                    for c in range(2):
                        chunk(c, c)
                    with engine.Fori(0, (NCH - 2) // 2) as j:
                        for u in range(2):
                            chunk(2 * j + 2 + u, u)

                with nc.Block() as block:
                    @block.sync
                    def _(sp):
                        sp.dma_start(gate[:], t[f"L{layer}_gateT"]).then_inc(params_in, 16)
                        sp.dma_start(gate_b[:], t["L0_gateB"]).then_inc(params_in, 16)

                    @block.gpsimd
                    def _(pool):
                        nc.gpsimd.memset(KEEP[:, :, 1:EXPERTS], 1.0)
                        nc.gpsimd.memset(KEEP[:, :, 0:1], 0.0).then_inc(keep_ready, 1)

                    @block.tensor
                    def _(pe):
                        pe.wait_ge(params_in, 32)

                        def chunk(c, u):
                            pe.wait_ge(xn_ready, 4 * c + 4)
                            need(pe, xt_ready, c - 1)
                            for k in range(4):
                                mm = nc.tensor.transpose(bank_t[u][:, P * k:P * k + P], XN[:, u, k, :], ident[:])
                            mm.then_inc(t_done, 1)

                        chunks(pe, chunk)
                        pe.wait_ge(xt_ready, NCH)
                        for b in range(B):
                            mm = nc.tensor.matmul(bank_l[:, EXPERTS * b:EXPERTS * b + EXPERTS], XT[:, b, :], gate[:],
                                                  start=True, stop=True)
                        mm.then_inc(lg_done, 1)

                    @block.scalar
                    def _(act):
                        def chunk(c, u):
                            act.wait_ge(t_done, c + 1)
                            nc.scalar.activation(XT[:, bass.ds(4 * c, 4), :], bank_t[u][:].rearrange("p (k c) -> p k c", k=4),
                                                 ACT.Copy).then_inc(xt_ready, 1)

                        chunks(act, chunk)
                        act.wait_ge(exp_in, 1)
                        nc.scalar.activation(PR[:], LG[:], ACT.Exp).then_inc(exp_out, 1)

                    @block.vector
                    def _(dve):
                        def chunk(c, u):
                            need(dve, t_done, c - 1)
                            for k in range(4):
                                nc.vector.tensor_scalar(XN[:, u, k, :], X[:, 4 * c + k, :],
                                                        mean[:, bass.ds(4 * c + k, 1)],
                                                        rstd[:, bass.ds(4 * c + k, 1)], ALU.subtract,
                                                        ALU.mult).then_inc(xn_ready, 1)

                        chunks(dve, chunk)
                        count = [0]

                        def then(ins):
                            count[0] += 1
                            ins.then_inc(chain, 1)
                            dve.wait_ge(chain, count[0])

                        V = nc.vector

                        def wide(a):
                            return a[:].unsqueeze(2).to_broadcast([P, B, EXPERTS])

                        dve.wait_ge(params_in, 32)
                        dve.wait_ge(keep_ready, 1)
                        dve.wait_ge(lg_done, 1)
                        logits = bank_l[:, 0:B * EXPERTS].rearrange("p (b e) -> p b e", e=EXPERTS)
                        if layer == 0:
                            then(V.tensor_tensor(T1[:], logits, gate_b[:].unsqueeze(1).to_broadcast([P, B, EXPERTS]), ALU.add))
                        else:
                            then(V.tensor_copy(T1[:], logits))
                        then(V.tensor_reduce(R1[:], T1[:], AX_X, ALU.max))
                        V.tensor_tensor(LG[:], T1[:], wide(R1), ALU.subtract).then_inc(exp_in, 1)
                        dve.wait_ge(exp_out, 1)
                        then(V.tensor_reduce(R1[:], PR[:], AX_X, ALU.add))
                        then(V.reciprocal(V1[:], R1[:]))
                        then(V.tensor_tensor(T1[:], PR[:], wide(V1), ALU.mult))
                        then(V.tensor_reduce(V1[:], T1[:], AX_X, ALU.max))
                        then(V.tensor_tensor(T2[:], T1[:], wide(V1), ALU.is_equal))
                        then(V.tensor_tensor_scan(T3[:].rearrange("p b e -> p (b e)"), KEEP[:].rearrange("p b e -> p (b e)"),
                                                  T2[:].rearrange("p b e -> p (b e)"), 0.0, ALU.mult, ALU.add))
                        then(V.scalar_tensor_tensor(T2[:], T3[:], 1.0, T2[:], ALU.is_equal, ALU.mult))
                        then(V.scalar_tensor_tensor(PR[:], T2[:], -2.0, T1[:], ALU.mult, ALU.add))
                        then(V.tensor_reduce(V2[:], PR[:], AX_X, ALU.max))
                        then(V.tensor_tensor(LG[:], PR[:], wide(V2), ALU.is_equal))
                        then(V.tensor_tensor_scan(T3[:].rearrange("p b e -> p (b e)"), KEEP[:].rearrange("p b e -> p (b e)"),
                                                  LG[:].rearrange("p b e -> p (b e)"), 0.0, ALU.mult, ALU.add))
                        then(V.scalar_tensor_tensor(LG[:], T3[:], 1.0, LG[:], ALU.is_equal, ALU.mult))
                        then(V.tensor_tensor(T2[:], T2[:], LG[:], ALU.add))
                        then(V.tensor_tensor(V1[:], V1[:], V2[:], ALU.add))
                        if layer == 0:
                            then(V.tensor_scalar(V1[:], V1[:], 1e-20, None, ALU.add))
                        then(V.reciprocal(V2[:], V1[:]))
                        then(V.tensor_tensor(T1[:], T1[:], T2[:], ALU.mult))
                        then(V.tensor_tensor(comb[:], T1[:], wide(V2), ALU.mult))

        def experts(layer):
            tag = f"F{layer}"
            tiles, F = (4, 102) if layer == 0 else (2, 128)
            KD = F + 1 if layer == 0 else F
            with ExitStack() as inner:
                def isb(name, shape):
                    return inner.enter_context(nc.sbuf_tensor(f"{name}_{tag}", shape, F32))

                def sem(name):
                    return inner.enter_context(nc.semaphore(f"{name}_{tag}"))

                gw = isb("gw", [D, EXPERTS, tiles, F])
                uw = isb("uw", [D, EXPERTS, tiles, F])
                dw = isb("dw", [KD, EXPERTS, tiles, D])
                gb = isb("gb", [F, EXPERTS * tiles])
                ub = isb("ub", [F, EXPERTS * tiles])
                GS = isb("GS", [P, 2, CH])
                HP = isb("HP", [P, 2, CH])
                H = isb("H", [P, 2, tiles, CH])
                params_in, ones_done = sem("params_in"), sem("ones_done")
                g_done, u_done, gs_ready, hp_ready, h_ready = (sem("g_done"), sem("u_done"), sem("gs_ready"),
                                                               sem("hp_ready"), sem("h_ready"))
                if layer == 1:
                    h_ready = hp_ready
                y_done, x_done = sem("y_done"), sem("x_done")
                bank_g, bank_u, bank_y = banks[0:2], banks[2:4], banks[4:6]
                NT = EXPERTS * tiles
                n_params = 5 if layer == 0 else 3

                with nc.Block() as block:
                    @block.sync
                    def _(sp):
                        sp.dma_start(gw[:], t[f"L{layer}_gpT"]).then_inc(params_in, 16)
                        sp.dma_start(uw[:], t[f"L{layer}_upT"]).then_inc(params_in, 16)
                        sp.dma_start(dw[:], t[f"L{layer}_downT"]).then_inc(params_in, 16)
                        if layer == 0:
                            sp.dma_start(gb[:], t["L0_gpB"]).then_inc(params_in, 16)
                            sp.dma_start(ub[:], t["L0_upB"]).then_inc(params_in, 16)

                    @block.gpsimd
                    def _(pool):
                        nc.gpsimd.memset(H[:], 1.0).then_inc(ones_done, 1)

                    @block.tensor
                    def _(pe):
                        pe.wait_ge(params_in, 16 * n_params)
                        pe.wait_ge(ones_done, 1)

                        def down(c, e, base):
                            pe.wait_ge(h_ready, base * NT + tiles * (e + 1))
                            if e >= 2:
                                pe.wait_ge(x_done, base * EXPERTS + e - 1)
                            elif not isinstance(base, int) or base:
                                pe.wait_ge(x_done, base * EXPERTS + e - 1)
                            for k in range(4):
                                for j in range(tiles):
                                    K = KD if j == 0 else F
                                    mm = nc.tensor.matmul(bank_y[e % 2][:, P * k:P * k + P],
                                                          H[0:K, e % 2, j, P * k:P * k + P], dw[0:K, e, j, :],
                                                          start=(j == 0), stop=(j == tiles - 1))
                            mm.then_inc(y_done, 1)

                        def chunk(c, base):
                            xs = XT[:, bass.ds(4 * c, 4), :]
                            for e in range(EXPERTS):
                                for j in range(tiles):
                                    m = e * tiles + j
                                    first = isinstance(base, int) and base == 0
                                    if m >= 2 or not first:
                                        pe.wait_ge(gs_ready, base * NT + m - 1)
                                    nc.tensor.matmul(bank_g[m % 2][0:F, :], gw[:, e, j, :], xs,
                                                     start=True, stop=True).then_inc(g_done, 1)
                                    if m >= 2 or not first:
                                        pe.wait_ge(hp_ready, base * NT + m - 1)
                                    nc.tensor.matmul(bank_u[m % 2][0:F, :], uw[:, e, j, :], xs,
                                                     start=True, stop=True).then_inc(u_done, 1)
                                if e >= 1:
                                    down(c, e - 1, base)
                            down(c, EXPERTS - 1, base)

                        chunk(0, 0)
                        with pe.Fori(1, NCH) as c:
                            chunk(c, c)

                    @block.scalar
                    def _(act):
                        if layer == 0:
                            act.wait_ge(params_in, 16 * n_params)
                        act.wait_ge(ones_done, 1)

                        def chunk(c, base):
                            first = isinstance(base, int) and base == 0
                            for m in range(NT + 1):
                                if m < NT:
                                    act.wait_ge(g_done, base * NT + m + 1)
                                    if m >= 2 or not first:
                                        act.wait_ge(hp_ready, base * NT + m - 1)
                                    if layer == 0:
                                        nc.scalar.activation(GS[0:F, m % 2, :], bank_g[m % 2][0:F, :], ACT.Identity,
                                                             bias=gb[:, m:m + 1]).then_inc(gs_ready, 1)
                                    else:
                                        nc.scalar.activation(GS[0:F, m % 2, :], bank_g[m % 2][0:F, :],
                                                             ACT.Silu).then_inc(gs_ready, 1)
                                if layer == 0 and m >= 1:
                                    k = m - 1
                                    e, j = k // tiles, k % tiles
                                    act.wait_ge(hp_ready, base * NT + k + 1)
                                    if j == 0 and (e >= 2 or not first):
                                        act.wait_ge(y_done, base * EXPERTS + e - 1)
                                    nc.scalar.activation(H[0:F, e % 2, j, :], HP[0:F, k % 2, :],
                                                         ACT.Silu).then_inc(h_ready, 1)

                        chunk(0, 0)
                        with act.Fori(1, NCH) as c:
                            chunk(c, c)

                    @block.vector
                    def _(dve):
                        if layer == 0:
                            dve.wait_ge(params_in, 16 * n_params)
                        dve.wait_ge(ones_done, 1)

                        def update(c, e, base):
                            dve.wait_ge(y_done, base * EXPERTS + e + 1)
                            for k in range(4):
                                if k == 0 and not (isinstance(base, int) and base == 0 and e == 0):
                                    dve.wait_ge(x_done, base * EXPERTS + e)
                                ins = nc.vector.scalar_tensor_tensor(
                                    X[:, 4 * c + k, :], bank_y[e % 2][:, P * k:P * k + P],
                                    comb[:, 4 * c + k, e:e + 1], X[:, 4 * c + k, :], ALU.mult, ALU.add)
                            ins.then_inc(x_done, 1)

                        def chunk(c, base):
                            first = isinstance(base, int) and base == 0
                            for m in range(NT):
                                e, j = m // tiles, m % tiles
                                dve.wait_ge(gs_ready, base * NT + m + 1)
                                dve.wait_ge(u_done, base * NT + m + 1)
                                if layer == 0:
                                    if m >= 2 or not first:
                                        dve.wait_ge(h_ready, base * NT + m - 1)
                                    nc.vector.scalar_tensor_tensor(HP[0:F, m % 2, :], bank_u[m % 2][0:F, :],
                                                                   ub[:, m:m + 1], GS[0:F, m % 2, :], ALU.add,
                                                                   ALU.mult).then_inc(hp_ready, 1)
                                else:
                                    if j == 0 and (e >= 2 or not first):
                                        dve.wait_ge(y_done, base * EXPERTS + e - 1)
                                    nc.vector.tensor_tensor(H[0:F, e % 2, j, :], bank_u[m % 2][0:F, :],
                                                            GS[0:F, m % 2, :], ALU.mult).then_inc(hp_ready, 1)
                                if e >= 1 and j == tiles - 1:
                                    update(c, e - 1, base)
                            update(c, EXPERTS - 1, base)

                        chunk(0, 0)
                        with dve.Fori(1, NCH) as c:
                            chunk(c, c)

        def store():
            with ExitStack() as sems:
                stored = sems.enter_context(nc.semaphore("stored"))
                with nc.Block() as block:
                    @block.sync
                    def _(sp):
                        sp.dma_start(t["out"].rearrange("b p d -> p b d"), X[:]).then_inc(stored, 16)
                        sp.wait_ge(stored, 16)

        load_constants()
        for layer in range(2):
            layer_norm_stats(f"A{layer}")
            attention(layer)
            layer_norm_stats(f"F{layer}")
            route(layer)
            experts(layer)
        store()


def _layouts(inputs):
    import numpy as np

    a = {k: np.asarray(v) for k, v in inputs.items()}
    out = {"x": a["x"], "ctx": a["ctx_1024"]}

    def heads_out(w):
        v = np.zeros((D, GROUPS, QUADS, SLOT), w.dtype)
        v[..., :HD] = w.T.reshape(D, GROUPS, QUADS, HD)
        return v.reshape(D, GROUPS, P)

    def heads_bias(b, one):
        v = np.zeros((QUADS, SLOT, GROUPS), b.dtype)
        v[:, :HD, :] = b.reshape(GROUPS, QUADS, HD).transpose(1, 2, 0)
        if one:
            v[:, HD, :] = 1
        return v.reshape(P, GROUPS)

    for n in range(2):
        p = f"L{n}_xattn_"
        out[f"L{n}_WqP"] = heads_out(a[p + "Wq"])
        out[f"L{n}_WkP"] = heads_out(a[p + "Wk"])
        out[f"L{n}_WvT"] = a[p + "Wv"].T
        out[f"L{n}_WoT"] = a[p + "Wo"].T
        out[f"L{n}_bqP"] = heads_bias(a[p + "bq"], False)
        out[f"L{n}_bkP"] = heads_bias(a[p + "bk"], True)
        out[f"L{n}_bvB"] = np.broadcast_to(a[p + "bv"], (P, D))
        out[f"L{n}_boB"] = np.broadcast_to(a[p + "bo"], (P, D))
    out["L0_gateT"] = a["L0_ffn_gate_w"].T
    out["L1_gateT"] = a["L1_ffn_wg"].T
    out["L0_gateB"] = np.broadcast_to(a["L0_ffn_gate_b"], (P, EXPERTS))
    for n, g, u, dn, tiles in ((0, "L0_ffn_gp_w", "L0_ffn_up_w", "L0_ffn_down_w", 4),
                               (1, "L1_ffn_w1", "L1_ffn_w3", "L1_ffn_w2", 2)):
        F = a[g].shape[1] // tiles
        out[f"L{n}_gpT"] = a[g].transpose(2, 0, 1).reshape(D, EXPERTS, tiles, F)
        out[f"L{n}_upT"] = a[u].transpose(2, 0, 1).reshape(D, EXPERTS, tiles, F)
        dT = a[dn].transpose(2, 0, 1).reshape(tiles, F, EXPERTS, D).transpose(1, 2, 0, 3)
        if n == 0:
            full = np.zeros((F + 1, EXPERTS, tiles, D), dT.dtype)
            full[:F] = dT
            full[F, :, 0, :] = a["L0_ffn_down_b"]
            dT = full
        out[f"L{n}_downT"] = dT
    out["L0_gpB"] = a["L0_ffn_gp_b"].reshape(EXPERTS * 4, 102).T
    out["L0_upB"] = a["L0_ffn_up_b"].reshape(EXPERTS * 4, 102).T
    return {k: np.ascontiguousarray(v) for k, v in out.items()}


def kernel(**inputs):
    import numpy as _np
    import concourse.bacc as _bacc
    from concourse import mybir as _mybir
    from concourse.bass_utils import run_bass_kernel_spmd as _run

    nc = _bacc.Bacc("TRN2", target_bir_lowering=False, num_devices=1)
    arrays, tensors = {}, {}
    for name, a in _layouts(inputs).items():
        arrays[f"in_{name}"] = a
        tensors[name] = nc.dram_tensor(f"in_{name}", a.shape, _mybir.dt.from_np(a.dtype), kind="ExternalInput").ap()
    shape = inputs["x"].shape
    tensors["out"] = nc.dram_tensor("out_x", shape, F32, kind="ExternalOutput").ap()
    build_program(nc, tensors)
    r = _run(nc, [arrays], core_ids=[0])
    return r.results[0]["out_x"]
```

```python
from contextlib import ExitStack

import concourse.bass as bass
from concourse import mybir

F32 = mybir.dt.float32
F32R = mybir.dt.float32r
ALU = mybir.AluOpType
ACT = mybir.ActivationFunctionType
BF16 = mybir.dt.bfloat16
I32 = mybir.dt.int32
AX_X = mybir.AxisListType.X

P = 128
D = 128
HEADS = 16
HD = D // HEADS
QUADS = 4
GROUPS = HEADS // QUADS
SLOT = 32
ONES = 3 * HD
EXPERTS = 8
EPS = 1e-5


def need(engine, semaphore, count):
    if not isinstance(count, int) or count > 0:
        engine.wait_ge(semaphore, count)


def build_program(nc, t):
    B = t["x"].shape[0]
    NCH = B // 4
    TOKENS = B * P
    SUBTILES = 2 * B + EXPERTS
    TRASH = 2 * TOKENS
    ROUND = float(3 * 2 ** 22)

    with ExitStack() as ctx:
        def sb(name, shape):
            return ctx.enter_context(nc.sbuf_tensor(name, shape, F32))

        banks = [ctx.enter_context(nc.psum_tensor(f"bank{i}", [P, 512], F32)) for i in range(8)]

        X = sb("X", [P, B, D])
        weight = sb("weight", [P, 2, B])
        ident = sb("ident", [P, P])
        mean = sb("mean", [P, B])
        rstd = sb("rstd", [P, B])
        minus_half = sb("minus_half", [P, B])
        earlier = sb("earlier", [P, P])
        ones = sb("ones", [P, P])
        count = sb("count", [P, P])
        count_p = sb("count_p", [P, 1])
        index = ctx.enter_context(nc.sbuf_tensor("index", [P, 2, SUBTILES], I32))
        expert_of = ctx.enter_context(nc.sbuf_tensor("expert_of", [P, SUBTILES], I32))

        xn_rows = nc.dram_tensor("xn_rows", [TOKENS, D], F32, kind="Internal").ap()
        results = nc.dram_tensor("results", [TRASH + SUBTILES * P, D], F32, kind="Internal").ap()

        QB = ctx.enter_context(nc.sbuf_tensor("QB", [P, 2, GROUPS, QUADS, P], F32R))
        KB = ctx.enter_context(nc.sbuf_tensor("KB", [P, 2, GROUPS, QUADS, P], F32R))

        def load_constants():
            with ExitStack() as sems:
                loaded = sems.enter_context(nc.semaphore("loaded_const"))
                zeroed = sems.enter_context(nc.semaphore("ident_zeroed"))
                count_i = sems.enter_context(nc.sbuf_tensor("count_i", [P, P], I32))
                count_pi = sems.enter_context(nc.sbuf_tensor("count_pi", [P, 1], I32))
                with nc.Block() as block:
                    @block.sync
                    def _(sp):
                        sp.dma_start(X[:], t["x"].rearrange("b p d -> p b d")).then_inc(loaded, 16)
                        sp.wait_ge(loaded, 16)

                    @block.gpsimd
                    def _(pool):
                        nc.gpsimd.memset(QB[:].bitcast(F32), 0.0)
                        nc.gpsimd.memset(KB[:].bitcast(F32), 0.0)
                        nc.gpsimd.memset(minus_half[:], -0.5)
                        nc.gpsimd.memset(ident[:], 0.0).then_inc(zeroed, 1)
                        nc.gpsimd.memset(ones[:], 1.0).then_inc(zeroed, 1)
                        nc.gpsimd.iota(count_i[:], [[1, P]], base=0, channel_multiplier=0).then_inc(zeroed, 1)
                        nc.gpsimd.iota(count_pi[:], [[1, 1]], base=1, channel_multiplier=1).then_inc(zeroed, 1)
                        pool.wait_ge(zeroed, 4)
                        nc.gpsimd.affine_select(out=ident[:], in_=ident[:], compare_op=ALU.not_equal, fill=1.0,
                                                base=0, pattern=[[-1, P]], channel_multiplier=1)
                        nc.gpsimd.affine_select(out=earlier[:], in_=ones[:], compare_op=ALU.is_gt, fill=0.0,
                                                base=0, pattern=[[1, P]], channel_multiplier=-1)
                        nc.gpsimd.tensor_copy(count[:], count_i[:])
                        nc.gpsimd.tensor_copy(count_p[:], count_pi[:])

        def layer_norm_stats(tag):
            with ExitStack() as inner:
                stats = inner.enter_context(nc.sbuf_tensor(f"stats_{tag}", [P, B, 6], F32))
                half = inner.enter_context(nc.sbuf_tensor(f"half_{tag}", [P, 3, B], F32))
                stats_done = inner.enter_context(nc.semaphore(f"stats_done_{tag}"))
                aggr_done = inner.enter_context(nc.semaphore(f"aggr_done_{tag}"))
                eps_done = inner.enter_context(nc.semaphore(f"eps_done_{tag}"))
                with nc.Block() as block:
                    @block.vector
                    def _(dve):
                        with dve.Fori(0, B) as b:
                            nc.vector.bn_stats(stats[:, b, :], X[:, b, :]).then_inc(stats_done, 1)
                        dve.wait_ge(stats_done, B)
                        V = nc.vector
                        mean_e, mean_o, sq_e, sq_o = (stats[:, :, k] for k in (1, 4, 2, 5))
                        V.tensor_tensor(half[:, 0, :], mean_e, mean_o, ALU.add).then_inc(aggr_done, 1)
                        V.tensor_tensor(half[:, 1, :], mean_e, mean_o, ALU.subtract).then_inc(aggr_done, 1)
                        V.tensor_tensor(half[:, 2, :], sq_e, sq_o, ALU.add).then_inc(aggr_done, 1)
                        dve.wait_ge(aggr_done, 3)
                        V.tensor_scalar(mean[:], half[:, 0, :], 0.5, None, ALU.mult).then_inc(aggr_done, 1)
                        V.scalar_tensor_tensor(half[:, 1, :], half[:, 1, :], 0.25, half[:, 1, :], ALU.mult,
                                               ALU.mult).then_inc(aggr_done, 1)
                        dve.wait_ge(aggr_done, 5)
                        V.scalar_tensor_tensor(rstd[:], half[:, 2, :], 1.0 / D, half[:, 1, :], ALU.mult,
                                               ALU.add).then_inc(aggr_done, 1)

                    @block.gpsimd
                    def _(pool):
                        pool.wait_ge(aggr_done, 6)
                        nc.gpsimd.tensor_scalar(rstd[:], rstd[:], 1.0, EPS, ALU.mult,
                                                ALU.add).then_inc(eps_done, 1)
                        pool.wait_ge(eps_done, 1)
                        nc.gpsimd.tensor_tensor(rstd[:], rstd[:], minus_half[:], ALU.pow)

        def attention(layer):
            tag = f"L{layer}"
            scale = (1.0 / D ** 0.5) if layer == 0 else HD ** -0.5
            with ExitStack() as inner:
                def isb(name, shape, dtype=F32):
                    return inner.enter_context(nc.sbuf_tensor(f"{name}_{tag}", shape, dtype))

                def sem(name):
                    return inner.enter_context(nc.semaphore(f"{name}_{tag}"))

                wq = isb("wq", [D, GROUPS, P])
                wk = isb("wk", [D, GROUPS, P])
                wv = isb("wv", [D, D])
                wo = isb("wo", [D, D])
                bq = isb("bq", [P, GROUPS])
                bk = isb("bk", [P, GROUPS])
                q_low = isb("q_low", [P, 1])
                k_low = isb("k_low", [P, 1])
                bv = isb("bv", [P, D])
                bo = isb("bo", [P, D])
                C = isb("C", [P, 4, D])
                XN = isb("XN", [P, 2, D])
                XB = isb("XB", [P, 2, D])
                XCT = isb("XCT", [D, 2, 2, P])
                ZQ = isb("ZQ", [P, 2, GROUPS, P])
                ZK = isb("ZK", [P, 2, GROUPS, P])
                HQ = isb("HQ", [P, 2, GROUPS, P], F32R)
                HK = isb("HK", [P, 2, GROUPS, P], F32R)
                QS = isb("QS", [P, 4, GROUPS, P], F32R)
                KS = isb("KS", [P, 4, GROUPS, P], F32R)
                QA = isb("QA", [P, 2, GROUPS, P], F32R)
                VA = isb("VA", [P, 4, HEADS, SLOT])
                NM = isb("NM", [P, 2, GROUPS, P])
                MX = isb("MX", [P, 2, HEADS])
                E = isb("E", [P, GROUPS, QUADS, P])
                OS = isb("OS", [P, 2, GROUPS, P])
                RD = isb("RD", [P, 2, HEADS])
                ON = isb("ON", [P, 2, D])
                ONT = isb("ONT", [D, 2, P])

                bank_t, bank_q, bank_k, bank_o = banks[0], banks[1], banks[2], banks[7]
                bank_s, bank_st = banks[3:5], banks[5:7]

                params_in = sem("params_in")
                ctx_in = [sem("ctx_in0"), sem("ctx_in1")]
                kb_in = [sem("kb_in0"), sem("kb_in1")]
                qb_in = [sem("qb_in0"), sem("qb_in1")]
                fill_done = sem("fill_done")
                xn_ready, xb_ready = sem("xn_ready"), sem("xb_ready")
                t_done, xct_ready = sem("t_done"), sem("xct_ready")
                q_done, k_done, v_done = sem("q_done"), sem("k_done"), sem("v_done")
                zq_ready, zk_ready, hq_ready, hk_ready = sem("zq_ready"), sem("zk_ready"), sem("hq_ready"), sem("hk_ready")
                q_ready, k_ready, v_ready = sem("q_ready"), sem("k_ready"), sem("v_ready")
                s_done, max_done, nh_ready, nm_ready = sem("s_done"), sem("max_done"), sem("nh_ready"), sem("nm_ready")
                mt_done, qa_ready = sem("mt_done"), sem("qa_ready")
                st_done, exp_done, pv_done, os_ready = sem("st_done"), sem("exp_done"), sem("pv_done"), sem("os_ready")
                ot_done, rd_ready, on_ready = sem("ot_done"), sem("rd_ready"), sem("on_ready")
                ont_done, ont_ready = sem("ont_done"), sem("ont_ready")
                out_done, x_done = sem("out_done"), sem("x_done")
                N_PARAMS = 10

                def pipeline(engine, step):
                    for n in range(-2, 4):
                        step(n, n % 4)
                    with engine.Fori(0, (B - 8) // 4) as j:
                        for r in range(4):
                            step(4 * j + 4 + r, r)
                    for n in range(B - 4, B + 3):
                        step(n, n % 4)

                def exists(n, ahead):
                    return not isinstance(n, int) or 0 <= n + ahead < B

                def loads(n, p):
                    return (n - p) * 8 + 16

                def by_head(a):
                    return a.rearrange("p (i k) -> p i k", i=QUADS)

                with nc.Block() as block:
                    @block.sync
                    def _(sp):
                        context = t["ctx"].rearrange("b p d -> p b d")
                        for dst, src in ((wq, "WqP"), (wk, "WkP"), (wv, "WvT"), (wo, "WoT"),
                                         (bq, "bqP"), (bk, "bkP"), (bv, "bvB"), (bo, "boB")):
                            sp.dma_start(dst[:], t[f"L{layer}_{src}"]).then_inc(params_in, 16)
                        sp.dma_start(q_low[:], t["q_low"]).then_inc(params_in, 16)
                        sp.dma_start(k_low[:], t["k_low"]).then_inc(params_in, 16)
                        for i in range(2):
                            sp.dma_start(C[:, 2 * i:2 * i + 2, :], context[:, 2 * i:2 * i + 2, :]).then_inc(ctx_in[i], 16)

                        def spread(dst, src, p, landed):
                            for i in range(QUADS):
                                rows = slice(SLOT * i, SLOT * i + SLOT)
                                sp.dma_start(dst[rows, p, :, i, :].bitcast(F32), src[rows, :, :].bitcast(F32)).then_inc(landed[p], 16)

                        def step(n, r):
                            p, q = r % 2, 1 - r % 2
                            if exists(n, 1):
                                sp.wait_ge(k_ready, n + 2)
                                spread(KB, KS[:, (r + 1) % 4, :, :], q, kb_in)
                            if exists(n, -1):
                                sp.wait_ge(qa_ready, n)
                                spread(QB, QA[:, q, :, :], q, qb_in)
                            if exists(n, 0) and exists(n, 4) and p == 0:
                                sp.wait_ge(t_done, n + 2)
                                sp.dma_start(C[:, r:r + 2, :], context[:, bass.ds(n + 4, 2), :]).then_inc(ctx_in[r // 2], 16)

                        pipeline(sp, step)

                    @block.gpsimd
                    def _(pool):
                        nc.gpsimd.memset(VA[:], 0.0).then_inc(fill_done, 1)
                        nc.gpsimd.memset(NM[:], 0.0).then_inc(fill_done, 1)
                        pool.wait_ge(fill_done, 2)
                        nc.gpsimd.memset(VA[:, :, :, HD:HD + 1], 1.0).then_inc(fill_done, 1)
                        pool.wait_ge(params_in, N_PARAMS * 16)

                        def step(n, r):
                            p, q = r % 2, 1 - r % 2
                            if exists(n, -2):
                                need(pool, x_done, n - 3)
                                nc.gpsimd.tensor_tensor(XB[:, p, :], X[:, n - 2, :], bo[:], ALU.add).then_inc(xb_ready, 1)
                            if exists(n, 2):
                                pool.wait_ge(zk_ready, n + 3)
                                need(pool, k_ready, n + 1)
                                nc.gpsimd.tensor_tensor(HK[:, p, :, :], ZK[:, p, :, :], k_low[:].unsqueeze(2).to_broadcast([P, GROUPS, P]),
                                                        ALU.mult).then_inc(hk_ready, 1)
                                pool.wait_ge(zq_ready, n + 3)
                                need(pool, q_ready, n + 1)
                                nc.gpsimd.tensor_tensor(HQ[:, p, :, :], ZQ[:, p, :, :], q_low[:].unsqueeze(2).to_broadcast([P, GROUPS, P]),
                                                        ALU.mult).then_inc(hq_ready, 1)

                        pipeline(pool, step)

                    @block.tensor
                    def _(pe):
                        pe.wait_ge(params_in, N_PARAMS * 16)
                        pe.wait_ge(fill_done, 3)

                        def project(bank, w, x):
                            for g in range(GROUPS):
                                mm = nc.tensor.matmul(bank[:, P * g:P * g + P], w[:, g, :], x, start=True, stop=True)
                            return mm

                        def scores(n, r, g):
                            if g == 0:
                                pe.wait_ge(q_ready, n + 1)
                                pe.wait_ge(kb_in[r % 2], 4 * loads(n, r % 2))
                            need(pe, max_done, 4 * n + g - 1)
                            nc.tensor.matmul(bank_s[g % 2][:], QS[:, r, g, :], KB[:, r % 2, g, :, :],
                                             start=True, stop=True).then_inc(s_done, 1)

                        def transposed_scores(m, r, g):
                            if g == 0:
                                pe.wait_ge(qb_in[r % 2], 4 * loads(m, r % 2))
                            need(pe, exp_done, 4 * m + g - 1)
                            nc.tensor.matmul(bank_st[g % 2][:], KS[:, (r + 2) % 4, g, :], QB[:, r % 2, g, :, :],
                                             start=True, stop=True).then_inc(st_done, 1)

                        def weigh(m, r, g):
                            pe.wait_ge(exp_done, 4 * m + g + 1)
                            if g == 0:
                                need(pe, os_ready, m)
                            for i in range(QUADS):
                                mm = nc.tensor.matmul(bank_o[SLOT * i:SLOT * i + SLOT, P * g:P * g + P],
                                                      VA[:, (r + 2) % 4, QUADS * g + i, :], E[:, g, i, :],
                                                      start=True, stop=True)
                            if g == GROUPS - 1:
                                mm.then_inc(pv_done, 1)

                        def step(n, r):
                            p, q = r % 2, 1 - r % 2
                            mid, back, tail = exists(n, 0), exists(n, -2), exists(n, -3)
                            if mid:
                                scores(n, r, 0)
                                scores(n, r, 1)
                            if exists(n, 1):
                                pe.wait_ge(xct_ready, n + 2)
                                need(pe, x_done, n - 3)
                                nc.tensor.matmul(bank_t[:, 0:P], XCT[:, q, 1, :], wv[:],
                                                 start=True, stop=True).then_inc(v_done, 1)
                            if exists(n, -1):
                                pe.wait_ge(nm_ready, n)
                                if exists(n, 1):
                                    pe.wait_ge(zq_ready, n + 2)
                                for g in range(GROUPS):
                                    mm = nc.tensor.transpose(bank_q[:, P * g:P * g + P], NM[:, q, g, :], ident[:])
                                mm.then_inc(mt_done, 1)
                            if back:
                                transposed_scores(n - 2, r, 0)
                            if exists(n, 2):
                                pe.wait_ge(xn_ready, n + 3)
                                s4 = (r + 2) % 4
                                pe.wait_ge(ctx_in[s4 // 2], (n + 2 - s4) * 4 + 16)
                                if exists(n, 1):
                                    pe.wait_ge(v_ready, n + 2)
                                nc.tensor.transpose(bank_t[:, 0:P], XN[:, p, :], ident[:])
                                nc.tensor.transpose(bank_t[:, P:2 * P], C[:, s4, :], ident[:]).then_inc(t_done, 1)
                            if tail:
                                pe.wait_ge(os_ready, n - 2)
                                if exists(n, 1):
                                    pe.wait_ge(zk_ready, n + 2)
                                for g in range(GROUPS):
                                    mm = nc.tensor.transpose(bank_k[:, P * g:P * g + P], OS[:, q, g, :], ident[:])
                                mm.then_inc(ot_done, 1)
                            if back:
                                transposed_scores(n - 2, r, 1)
                            if mid:
                                scores(n, r, 2)
                            if back:
                                transposed_scores(n - 2, r, 2)
                                weigh(n - 2, r, 0)
                            if tail:
                                pe.wait_ge(on_ready, n - 2)
                                if exists(n, 2):
                                    pe.wait_ge(xct_ready, n + 3)
                                elif exists(n, 1):
                                    pe.wait_ge(v_ready, n + 2)
                                nc.tensor.transpose(bank_t[:, 0:P], ON[:, q, :], ident[:]).then_inc(ont_done, 1)
                            if exists(n, 2):
                                pe.wait_ge(xct_ready, n + 3)
                                if not tail and exists(n, 1):
                                    pe.wait_ge(zk_ready, n + 2)
                                project(bank_k, wk, XCT[:, p, 1, :]).then_inc(k_done, 1)
                            if mid:
                                scores(n, r, 3)
                            if back:
                                transposed_scores(n - 2, r, 3)
                                weigh(n - 2, r, 1)
                            if tail:
                                pe.wait_ge(ont_ready, n - 2)
                                nc.tensor.matmul(bank_t[:, 0:P], ONT[:, q, :], wo[:],
                                                 start=True, stop=True).then_inc(out_done, 1)
                            if back:
                                weigh(n - 2, r, 2)
                            if exists(n, 2):
                                need(pe, qa_ready, n)
                                if not exists(n, -1) and exists(n, 1):
                                    pe.wait_ge(zq_ready, n + 2)
                                project(bank_q, wq, XCT[:, p, 0, :]).then_inc(q_done, 1)
                            if back:
                                weigh(n - 2, r, 3)

                        pipeline(pe, step)

                    @block.scalar
                    def _(act):
                        act.wait_ge(params_in, N_PARAMS * 16)

                        def exponentials(m, g):
                            act.wait_ge(st_done, 4 * m + g + 1)
                            if g == 0:
                                need(act, pv_done, m)
                            nc.scalar.activation(E[:, g, :, :], by_head(bank_st[g % 2][:]), ACT.Exp,
                                                 scale=scale).then_inc(exp_done, 1)

                        def bias_add(m, u, bank, Z, b, done, ready, used):
                            act.wait_ge(done, m + 1)
                            need(act, used, m - 1)
                            for g in range(GROUPS):
                                ins = nc.scalar.activation(Z[:, u, g, :], bank[:, P * g:P * g + P], ACT.Identity,
                                                           bias=b[:, g:g + 1])
                            ins.then_inc(ready, 1)

                        def step(n, r):
                            p, q = r % 2, 1 - r % 2
                            if exists(n, -2):
                                exponentials(n - 2, 0)
                            if exists(n, 2):
                                act.wait_ge(t_done, n + 3)
                                need(act, v_done, n + 1)
                                nc.scalar.activation(XCT[:, p, :, :], bank_t[:, 0:2 * P].rearrange("p (a b) -> p a b", a=2),
                                                     ACT.Copy).then_inc(xct_ready, 1)
                            if exists(n, -2):
                                exponentials(n - 2, 1)
                                exponentials(n - 2, 2)
                            if exists(n, -3):
                                act.wait_ge(ont_done, n - 2)
                                need(act, out_done, n - 4)
                                nc.scalar.activation(ONT[:, q, :], bank_t[:, 0:P], ACT.Copy).then_inc(ont_ready, 1)
                            if exists(n, 2):
                                bias_add(n + 2, p, bank_k, ZK, bk, k_done, zk_ready, k_ready)
                            if exists(n, -2):
                                exponentials(n - 2, 3)
                            if exists(n, 2):
                                bias_add(n + 2, p, bank_q, ZQ, bq, q_done, zq_ready, q_ready)
                            if exists(n, -2):
                                act.wait_ge(pv_done, n - 1)
                                need(act, ot_done, n - 3)
                                nc.scalar.activation(OS[:, p, :, :], bank_o[:].rearrange("p (g k) -> p g k", g=GROUPS),
                                                     ACT.Copy).then_inc(os_ready, 1)

                        pipeline(act, step)

                    @block.vector
                    def _(dve):
                        dve.wait_ge(params_in, N_PARAMS * 16)
                        dve.wait_ge(fill_done, 3)

                        def maximum(n, p, g):
                            dve.wait_ge(s_done, 4 * n + g + 1)
                            nc.vector.tensor_reduce(MX[:, p, QUADS * g:QUADS * g + QUADS], by_head(bank_s[g % 2][:]),
                                                    AX_X, ALU.max).then_inc(max_done, 1)

                        def step(n, r):
                            p, q = r % 2, 1 - r % 2
                            mid = exists(n, 0)
                            if exists(n, 2):
                                need(dve, t_done, n + 1)
                                nc.vector.tensor_scalar(XN[:, p, :], X[:, n + 2, :], mean[:, bass.ds(n + 2, 1)],
                                                        rstd[:, bass.ds(n + 2, 1)], ALU.subtract,
                                                        ALU.mult).then_inc(xn_ready, 1)
                            if exists(n, 1):
                                need(dve, pv_done, n - 2)
                                dve.wait_ge(hk_ready, n + 2)
                                nc.vector.tensor_tensor(KS[:, (r + 1) % 4, :, :], ZK[:, q, :, :], HK[:, q, :, :].bitcast(F32),
                                                        ALU.subtract).then_inc(k_ready, 1)
                            if mid:
                                maximum(n, p, 0)
                            if exists(n, 1):
                                dve.wait_ge(v_done, n + 2)
                                nc.vector.tensor_tensor(VA[:, (r + 1) % 4, :, 0:HD], bank_t[:, 0:P].rearrange("p (h d) -> p h d", h=HEADS),
                                                        bv[:].rearrange("p (h d) -> p h d", h=HEADS),
                                                        ALU.add).then_inc(v_ready, 1)
                            if exists(n, -1):
                                dve.wait_ge(mt_done, n)
                                if exists(n, -3):
                                    dve.wait_ge(qb_in[q], 4 * loads(n - 3, q))
                                nc.vector.tensor_tensor(QA[:, q, :, :], bank_q[:].rearrange("p (g k) -> p g k", g=GROUPS),
                                                        QS[:, (r + 3) % 4, :, :].bitcast(F32), ALU.add).then_inc(qa_ready, 1)
                            if exists(n, -3):
                                dve.wait_ge(ot_done, n - 2)
                                outs = bank_k[:].rearrange("p (h c) -> p h c", c=SLOT)
                                nc.vector.reciprocal(RD[:, q, :].rearrange("p (h o) -> p h o", o=1),
                                                     outs[:, :, HD:HD + 1]).then_inc(rd_ready, 1)
                                dve.wait_ge(rd_ready, n - 2)
                                need(dve, ont_done, n - 4)
                                nc.vector.tensor_tensor(ON[:, q, :].rearrange("p (h d) -> p h d", h=HEADS),
                                                        outs[:, :, 0:HD],
                                                        RD[:, q, :].unsqueeze(2).to_broadcast([P, HEADS, HD]),
                                                        ALU.mult).then_inc(on_ready, 1)
                            if mid:
                                maximum(n, p, 1)
                                maximum(n, p, 2)
                            if exists(n, 1):
                                dve.wait_ge(hq_ready, n + 2)
                                nc.vector.tensor_tensor(QS[:, (r + 1) % 4, :, :], ZQ[:, q, :, :], HQ[:, q, :, :].bitcast(F32),
                                                        ALU.subtract).then_inc(q_ready, 1)
                            if mid:
                                maximum(n, p, 3)
                                dve.wait_ge(max_done, 4 * n + 4)
                                maxima = MX[:, p, :].rearrange("p (g i) -> p g i", g=GROUPS)
                                high = NM[:, p, :, ONES:P:SLOT]
                                nc.vector.tensor_scalar(high.bitcast(F32R), maxima, -1.0, None, ALU.mult).then_inc(nh_ready, 1)
                            if exists(n, -3):
                                dve.wait_ge(out_done, n - 2)
                                dve.wait_ge(xb_ready, n - 2)
                                nc.vector.tensor_tensor(X[:, n - 3, :], bank_t[:, 0:P], XB[:, q, :],
                                                        ALU.add).then_inc(x_done, 1)
                            if mid:
                                dve.wait_ge(nh_ready, n + 1)
                                nc.vector.scalar_tensor_tensor(NM[:, p, :, ONES + 1:P:SLOT].bitcast(F32R), maxima, -1.0,
                                                               high, ALU.mult, ALU.subtract).then_inc(nm_ready, 1)

                        pipeline(dve, step)

        def route(layer):
            tag = f"R{layer}"
            with ExitStack() as inner:
                def isb(name, shape, dtype=F32):
                    return inner.enter_context(nc.sbuf_tensor(f"{name}_{tag}", shape, dtype))

                def sem(name):
                    return inner.enter_context(nc.semaphore(f"{name}_{tag}"))

                gate = isb("gate", [D, EXPERTS])
                gate_b = isb("gate_b", [P, EXPERTS])
                XN = isb("XN", [P, 2, 4, D])
                XT = isb("XT", [D, B, P])
                LG = isb("LG", [P, B, EXPERTS])
                PR = isb("PR", [P, B, EXPERTS])
                T1 = isb("T1", [P, B, EXPERTS])
                T2 = isb("T2", [P, B, EXPERTS])
                T3 = isb("T3", [P, B, EXPERTS])
                R1 = isb("R1", [P, B])
                V1 = isb("V1", [P, B])
                V2 = isb("V2", [P, B])
                KEEP = isb("KEEP", [P, B, EXPERTS])
                KEEPB = isb("KEEPB", [P, EXPERTS, B])
                TOT = isb("TOT", [P, EXPERTS, B])
                BEFORE = isb("BEFORE", [P, EXPERTS, B])
                OVER = isb("OVER", [P, EXPERTS, B])
                EDGE = isb("EDGE", [P, B])
                tiles_of = isb("tiles_of", [P, EXPERTS])
                tiles_to = isb("tiles_to", [P, EXPERTS])
                SLOT_OF = isb("SLOT_OF", [P, 2 * B])
                HI = isb("HI", [P, 2 * B])
                LO = isb("LO", [P, 2 * B])
                AT_LO = isb("AT_LO", [P, 2 * B, P], BF16)
                AT_HI = isb("AT_HI", [P, 2 * B, SUBTILES], BF16)
                WHO = isb("WHO", [P, 2 * B, 2, SUBTILES], BF16)
                IDS = isb("IDS", [P, 2, SUBTILES])
                UNUSED = isb("UNUSED", [P, SUBTILES])
                ROW = isb("ROW", [P, 2, SUBTILES])
                PASTEND = isb("PASTEND", [P, SUBTILES])
                PAST = isb("PAST", [P, SUBTILES, EXPERTS - 1])
                bank_t, bank_l, bank_r, bank_n, bank_i = banks[0:2], banks[2], banks[3], banks[4], banks[5]
                params_in = sem("params_in")
                xn_ready, t_done, xt_ready = sem("xn_ready"), sem("t_done"), sem("xt_ready")
                lg_done, chain, exp_in, exp_out = sem("lg_done"), sem("chain"), sem("exp_in"), sem("exp_out")
                keep_ready, picked, counted, placed = sem("keep_ready"), sem("picked"), sem("counted"), sem("placed")
                rows_out = [sem("rows_out0"), sem("rows_out1")]
                past_part = sem("past_part")
                lo_ready, hi_ready, who_ready, ids_done = (sem("lo_ready"), sem("hi_ready"),
                                                                     sem("who_ready"), sem("ids_done"))

                def chunks(engine, chunk):
                    for c in range(2):
                        chunk(c, c)
                    with engine.Fori(0, (NCH - 2) // 2) as j:
                        for u in range(2):
                            chunk(2 * j + 2 + u, u)

                with nc.Block() as block:
                    @block.sync
                    def _(sp):
                        sp.dma_start(gate[:], t[f"L{layer}_gateT"]).then_inc(params_in, 16)
                        sp.dma_start(gate_b[:], t["L0_gateB"]).then_inc(params_in, 16)
                        rows = xn_rows.rearrange("(b p) d -> p b d", p=P)

                        def chunk(c, u):
                            sp.wait_ge(xn_ready, 4 * c + 4)
                            sp.dma_start(rows[:, bass.ds(4 * c, 4), :], XN[:, u, :, :]).then_inc(rows_out[u], 16)

                        chunks(sp, chunk)
                        for u in range(2):
                            sp.wait_ge(rows_out[u], 16 * NCH // 2)

                    @block.gpsimd
                    def _(pool):
                        nc.gpsimd.memset(KEEP[:, :, 1:EXPERTS], 1.0)
                        nc.gpsimd.memset(KEEP[:, :, 0:1], 0.0).then_inc(keep_ready, 1)
                        nc.gpsimd.memset(KEEPB[:, :, 1:B], 1.0)
                        nc.gpsimd.memset(KEEPB[:, :, 0:1], 0.0)
                        nc.gpsimd.tensor_scalar(PASTEND[:], count[:, 0:SUBTILES], float(P), float(TRASH), ALU.mult,
                                                ALU.add).then_inc(past_part, 1)
                        pool.wait_ge(past_part, 1)
                        nc.gpsimd.tensor_tensor(PASTEND[:], PASTEND[:], count_p[:].to_broadcast([P, SUBTILES]), ALU.add)
                        nc.gpsimd.tensor_scalar(EDGE[:], count[:, 0:B], float(P), None, ALU.mult).then_inc(keep_ready, 1)
                        pool.wait_ge(hi_ready, 1)
                        nc.gpsimd.tensor_tensor(WHO[:, :, 1, :], AT_HI[:],
                                                count[:, 0:2 * B].unsqueeze(2).to_broadcast([P, 2 * B, SUBTILES]), ALU.mult).then_inc(who_ready, 1)

                    @block.tensor
                    def _(pe):
                        pe.wait_ge(params_in, 32)

                        def chunk(c, u):
                            pe.wait_ge(xn_ready, 4 * c + 4)
                            need(pe, xt_ready, c - 1)
                            for k in range(4):
                                mm = nc.tensor.transpose(bank_t[u][:, P * k:P * k + P], XN[:, u, k, :], ident[:])
                            mm.then_inc(t_done, 1)

                        chunks(pe, chunk)
                        pe.wait_ge(xt_ready, NCH)
                        for b in range(B):
                            mm = nc.tensor.matmul(bank_l[:, EXPERTS * b:EXPERTS * b + EXPERTS], XT[:, b, :], gate[:],
                                                  start=True, stop=True)
                        mm.then_inc(lg_done, 1)
                        pe.wait_ge(picked, 1)
                        chosen = T2[:].rearrange("p b e -> p (b e)")
                        nc.tensor.matmul(bank_r[:, 0:B * EXPERTS], earlier[:], chosen, start=True, stop=True)
                        nc.tensor.matmul(bank_n[:, 0:B * EXPERTS], ones[:], chosen, start=True, stop=True).then_inc(counted, 1)
                        pe.wait_ge(lo_ready, 2)
                        pe.wait_ge(who_ready, 2)
                        for k in range(2 * B):
                            mm = nc.tensor.matmul(bank_i[:, 0:2 * SUBTILES], AT_LO[:, k, :], WHO[:, k, :, :],
                                                  start=(k == 0), stop=(k == 2 * B - 1))
                        mm.then_inc(ids_done, 1)

                    @block.scalar
                    def _(act):
                        def chunk(c, u):
                            act.wait_ge(t_done, c + 1)
                            nc.scalar.activation(XT[:, bass.ds(4 * c, 4), :], bank_t[u][:].rearrange("p (k c) -> p k c", k=4),
                                                 ACT.Copy).then_inc(xt_ready, 1)

                        chunks(act, chunk)
                        act.wait_ge(exp_in, 1)
                        nc.scalar.activation(PR[:], LG[:], ACT.Exp).then_inc(exp_out, 1)
                        act.wait_ge(hi_ready, 1)
                        nc.scalar.activation(WHO[:, :, 0, :], AT_HI[:], ACT.Copy, scale=count_p[:]).then_inc(who_ready, 1)

                    @block.vector
                    def _(dve):
                        def chunk(c, u):
                            need(dve, t_done, c - 1)
                            if not isinstance(c, int) or c >= 2:
                                dve.wait_ge(rows_out[u], (c - u) * 8)
                            for k in range(4):
                                nc.vector.tensor_scalar(XN[:, u, k, :], X[:, 4 * c + k, :],
                                                        mean[:, bass.ds(4 * c + k, 1)],
                                                        rstd[:, bass.ds(4 * c + k, 1)], ALU.subtract,
                                                        ALU.mult).then_inc(xn_ready, 1)

                        chunks(dve, chunk)
                        chained = [0]

                        def then(ins):
                            chained[0] += 1
                            ins.then_inc(chain, 1)
                            dve.wait_ge(chain, chained[0])

                        V = nc.vector

                        def wide(a):
                            return a[:].unsqueeze(2).to_broadcast([P, B, EXPERTS])

                        dve.wait_ge(params_in, 32)
                        dve.wait_ge(keep_ready, 2)
                        dve.wait_ge(lg_done, 1)
                        logits = bank_l[:, 0:B * EXPERTS].rearrange("p (b e) -> p b e", e=EXPERTS)
                        if layer == 0:
                            then(V.tensor_tensor(T1[:], logits, gate_b[:].unsqueeze(1).to_broadcast([P, B, EXPERTS]), ALU.add))
                        else:
                            then(V.tensor_copy(T1[:], logits))
                        then(V.tensor_reduce(R1[:], T1[:], AX_X, ALU.max))
                        V.tensor_tensor(LG[:], T1[:], wide(R1), ALU.subtract).then_inc(exp_in, 1)
                        dve.wait_ge(exp_out, 1)
                        then(V.tensor_reduce(R1[:], PR[:], AX_X, ALU.add))
                        then(V.reciprocal(V1[:], R1[:]))
                        then(V.tensor_tensor(T1[:], PR[:], wide(V1), ALU.mult))
                        then(V.tensor_reduce(V1[:], T1[:], AX_X, ALU.max))
                        then(V.tensor_tensor(T2[:], T1[:], wide(V1), ALU.is_equal))
                        then(V.tensor_tensor_scan(T3[:].rearrange("p b e -> p (b e)"), KEEP[:].rearrange("p b e -> p (b e)"),
                                                  T2[:].rearrange("p b e -> p (b e)"), 0.0, ALU.mult, ALU.add))
                        then(V.scalar_tensor_tensor(T2[:], T3[:], 1.0, T2[:], ALU.is_equal, ALU.mult))
                        then(V.scalar_tensor_tensor(PR[:], T2[:], -2.0, T1[:], ALU.mult, ALU.add))
                        then(V.tensor_reduce(V2[:], PR[:], AX_X, ALU.max))
                        then(V.tensor_tensor(LG[:], PR[:], wide(V2), ALU.is_equal))
                        then(V.tensor_tensor_scan(T3[:].rearrange("p b e -> p (b e)"), KEEP[:].rearrange("p b e -> p (b e)"),
                                                  LG[:].rearrange("p b e -> p (b e)"), 0.0, ALU.mult, ALU.add))
                        then(V.scalar_tensor_tensor(LG[:], T3[:], 1.0, LG[:], ALU.is_equal, ALU.mult))
                        then(V.tensor_copy(PR[:], T2[:]))
                        V.tensor_tensor(T2[:], T2[:], LG[:], ALU.add).then_inc(picked, 1)
                        then(V.tensor_tensor(R1[:], V1[:], V2[:], ALU.add))
                        if layer == 0:
                            then(V.tensor_scalar(R1[:], R1[:], 1e-20, None, ALU.add))
                        then(V.reciprocal(R1[:], R1[:]))
                        then(V.tensor_tensor(weight[:, 0, :], V1[:], R1[:], ALU.mult))
                        then(V.tensor_tensor(weight[:, 1, :], V2[:], R1[:], ALU.mult))

                        def flat(a):
                            return a[:].rearrange("p e b -> p (e b)")

                        def by_expert(bank):
                            return bank[:, 0:B * EXPERTS].rearrange("p (b e) -> p e b", e=EXPERTS)

                        def over_batches(a):
                            return a[:].unsqueeze(2).to_broadcast([P, EXPERTS, B])

                        dve.wait_ge(counted, 1)
                        then(V.tensor_copy(TOT[:], by_expert(bank_n)))
                        then(V.tensor_tensor_scan(flat(BEFORE), flat(KEEPB), flat(TOT), 0.0, ALU.mult, ALU.add))
                        then(V.tensor_tensor(OVER[:], BEFORE[:, :, B - 1:B].to_broadcast([P, EXPERTS, B]),
                                             EDGE[:].unsqueeze(1).to_broadcast([P, EXPERTS, B]), ALU.is_gt))
                        then(V.tensor_reduce(tiles_of[:], OVER[:], AX_X, ALU.add))
                        then(V.tensor_tensor_scan(tiles_to[:], ones[:, 0:EXPERTS], tiles_of[:], 0.0, ALU.mult, ALU.add))
                        then(V.tensor_tensor(BEFORE[:], BEFORE[:], TOT[:], ALU.subtract))
                        then(V.tensor_tensor(tiles_of[:], tiles_to[:], tiles_of[:], ALU.subtract))
                        then(V.scalar_tensor_tensor(BEFORE[:], over_batches(tiles_of), float(P), BEFORE[:], ALU.mult, ALU.add))
                        then(V.tensor_tensor(BEFORE[:], BEFORE[:], by_expert(bank_r), ALU.add))
                        slots = BEFORE[:].rearrange("p e b -> p b e")
                        then(V.tensor_tensor(PR[:], PR[:], slots, ALU.mult))
                        then(V.tensor_tensor(LG[:], LG[:], slots, ALU.mult))
                        then(V.tensor_reduce(SLOT_OF[:, 0:B], PR[:], AX_X, ALU.add))
                        then(V.tensor_reduce(SLOT_OF[:, B:2 * B], LG[:], AX_X, ALU.add))
                        then(V.tensor_scalar(HI[:], SLOT_OF[:], 1.0 / P, -(P - 1) / (2.0 * P), ALU.mult, ALU.add))
                        then(V.tensor_scalar(HI[:], HI[:], ROUND, None, ALU.add))
                        then(V.tensor_scalar(HI[:], HI[:], ROUND, None, ALU.subtract))
                        V.scalar_tensor_tensor(LO[:], HI[:], -float(P), SLOT_OF[:], ALU.mult, ALU.add).then_inc(placed, 1)
                        V.tensor_tensor(AT_HI[:], count[:, 0:SUBTILES].unsqueeze(1).to_broadcast([P, 2 * B, SUBTILES]),
                                        HI[:].unsqueeze(2).to_broadcast([P, 2 * B, SUBTILES]), ALU.is_equal).then_inc(hi_ready, 1)
                        dve.wait_ge(placed, 1)
                        for c in range(2):
                            half = slice(B * c, B * c + B)
                            V.tensor_tensor(AT_LO[:, half, :], count[:].unsqueeze(1).to_broadcast([P, B, P]),
                                            LO[:, half].unsqueeze(2).to_broadcast([P, B, P]), ALU.is_equal).then_inc(lo_ready, 1)
                        then(V.tensor_tensor(PAST[:], count[:, 0:SUBTILES].unsqueeze(2).to_broadcast([P, SUBTILES, EXPERTS - 1]),
                                             tiles_to[:, 0:EXPERTS - 1].unsqueeze(1).to_broadcast([P, SUBTILES, EXPERTS - 1]),
                                             ALU.is_ge))
                        then(V.tensor_reduce(UNUSED[:], PAST[:], AX_X, ALU.add))
                        then(V.tensor_copy(expert_of[:], UNUSED[:]))
                        dve.wait_ge(ids_done, 1)
                        then(V.tensor_copy(IDS[:], bank_i[:, 0:2 * SUBTILES].rearrange("p (a k) -> p a k", a=2)))
                        then(V.tensor_scalar(UNUSED[:], IDS[:, 0, :], 0.5, None, ALU.is_lt))
                        then(V.scalar_tensor_tensor(IDS[:, 0, :], IDS[:, 1, :], float(P), IDS[:, 0, :], ALU.mult, ALU.add))
                        then(V.tensor_tensor(ROW[:, 1, :], UNUSED[:], PASTEND[:], ALU.mult))
                        then(V.scalar_tensor_tensor(ROW[:, 1, :], IDS[:, 0, :], 1.0, ROW[:, 1, :], ALU.subtract, ALU.add))
                        then(V.tensor_scalar(ROW[:, 0, :], IDS[:, 0, :], TOKENS + 0.5, -float(TOKENS), ALU.is_ge, ALU.mult))
                        then(V.tensor_tensor(ROW[:, 0, :], ROW[:, 0, :], IDS[:, 0, :], ALU.add))
                        then(V.tensor_scalar(UNUSED[:], UNUSED[:], count_p[:], -1.0, ALU.mult, ALU.add))
                        then(V.tensor_tensor(ROW[:, 0, :], ROW[:, 0, :], UNUSED[:], ALU.add))
                        then(V.tensor_copy(index[:], ROW[:]))

        def experts(layer):
            tag = f"F{layer}"
            tiles, F = (4, 102) if layer == 0 else (2, 128)
            W = tiles * F
            KD = F + 1 if layer == 0 else F
            with ExitStack() as inner:
                def isb(name, shape, dtype=F32):
                    return inner.enter_context(nc.sbuf_tensor(f"{name}_{tag}", shape, dtype))

                def sem(name):
                    return inner.enter_context(nc.semaphore(f"{name}_{tag}"))

                w_low = isb("w_low", [D, 2, EXPERTS, W], F32R)
                w_high = isb("w_high", [D, 2, EXPERTS, W], F32R)
                dw = isb("dw", [KD, EXPERTS, tiles, D])
                XG = isb("XG", [P, 4, D])
                XH = isb("XH", [D, 4, P], F32R)
                XL = isb("XL", [D, 4, P], F32R)
                GS = isb("GS", [P, 2, W])
                US = isb("US", [P, 2, W])
                H = isb("H", [P, 2, W])
                HT = isb("HT", [P, 2, tiles, P])
                Y = isb("Y", [P, 4, D])
                if layer == 0:
                    bias = isb("bias", [P, 2, EXPERTS, W])
                    HP = isb("HP", [P, 2, W])
                params_in, ones_done = sem("params_in"), sem("ones_done")
                high_ready, low_ready = sem("high_ready"), sem("low_ready")
                xg_in = [sem(f"xg_in{i}") for i in range(4)]
                y_out = [sem(f"y_out{i}") for i in range(4)]
                t_done, xh_ready, xl_ready = sem("t_done"), sem("xh_ready"), sem("xl_ready")
                g_done, u_done, gs_ready, us_ready = sem("g_done"), sem("u_done"), sem("gs_ready"), sem("us_ready")
                hp_ready, h_ready = sem("hp_ready"), sem("h_ready")
                if layer == 1:
                    h_ready = us_ready
                ht_done, ht_ready, y_done, y_ready = sem("ht_done"), sem("ht_ready"), sem("y_done"), sem("y_ready")
                bank_t, bank_ht = banks[0], banks[1]
                bank_g, bank_u, bank_y = banks[2:4], banks[4:6], banks[6:8]
                N_PARAMS = 4 if layer == 0 else 3
                S = SUBTILES

                def pipeline(engine, step):
                    for n in range(-2, 8):
                        step(n, n % 4)
                    with engine.Fori(0, (S - 12) // 4) as j:
                        for r in range(4):
                            step(4 * j + 8 + r, r)
                    for n in range(S - 4, S + 2):
                        step(n, n % 4)

                def exists(n, ahead):
                    return not isinstance(n, int) or 0 <= n + ahead < S

                def ring(n, r):
                    return (n - r) * 4 + 16

                with nc.Block() as block:
                    @block.sync
                    def _(sp):
                        for i, name in enumerate(("gpT", "upT")):
                            sp.dma_start(w_low[:, i, :, :].bitcast(F32), t[f"L{layer}_{name}"]).then_inc(params_in, 16)
                        sp.dma_start(dw[:], t[f"L{layer}_downT"]).then_inc(params_in, 16)
                        if layer == 0:
                            sp.dma_start(bias[:], t["L0_biasB"]).then_inc(params_in, 16)

                    @block.gpsimd
                    def _(pool):
                        nc.gpsimd.memset(HT[:], 1.0).then_inc(ones_done, 1)

                        def gather(n):
                            need(pool, t_done, n - 3)
                            pool.indirect_dma_start(XG[:, n % 4, :], None, xn_rows,
                                                    bass.IndirectOffsetOnAxis(index[:, 0, n:n + 1], 0)).then_inc(xg_in[n % 4], 16)

                        def scatter(n):
                            pool.wait_ge(y_ready, n + 1)
                            pool.indirect_dma_start(results, bass.IndirectOffsetOnAxis(index[:, 1, n:n + 1], 0),
                                                    Y[:, n % 4, :], None).then_inc(y_out[n % 4], 16)

                        for n in range(S + 3):
                            if n < S:
                                gather(n)
                            if n >= 3 + 3:
                                scatter(n - 6)
                        for n in range(S - 3, S):
                            scatter(n)
                        for i in range(4):
                            pool.wait_ge(y_out[i], 16 * S // 4)

                    @block.tensor
                    def _(pe):
                        pe.wait_ge(high_ready, 1)
                        pe.wait_ge(low_ready, 1)
                        pe.wait_ge(ones_done, 1)

                        held = {}

                        def expert(n):
                            return pe.value_load(expert_of[0:1, bass.ds(n, 1)], min_val=0, max_val=EXPERTS - 1)

                        def step(n, r):
                            u, v = r % 2, 1 - r % 2
                            if exists(n, 0):
                                e = held[r] = expert(n)
                                pe.wait_ge(xl_ready, n + 1)
                                for i, (bank, free, done) in enumerate(((bank_g[u], gs_ready, g_done),
                                                                        (bank_u[u], us_ready, u_done))):
                                    need(pe, free, n - 1)
                                    for k, (x, w) in enumerate(((XH, w_high), (XL, w_high), (XH, w_low))):
                                        mm = nc.tensor.matmul(bank[:, 0:W], x[:, r, :], w[:, i, e, :], start=(k == 0), stop=(k == 2))
                                    mm.then_inc(done, 1)
                            if exists(n, 2):
                                pe.wait_ge(xg_in[(r + 2) % 4], ring(n + 2, (r + 2) % 4))
                                need(pe, xl_ready, n + 2)
                                nc.tensor.transpose(bank_t[:, 0:P], XG[:, (r + 2) % 4, :], ident[:]).then_inc(t_done, 1)
                            if exists(n, -2):
                                e = held[(r + 2) % 4] if isinstance(n, int) or r >= 2 else expert(n - 2)
                                pe.wait_ge(ht_ready, n - 1)
                                need(pe, y_ready, n - 3)
                                for j in range(tiles):
                                    K = KD if j == 0 else F
                                    mm = nc.tensor.matmul(bank_y[u][:, 0:D], HT[0:K, u, j, :], dw[0:K, e, j, :],
                                                          start=(j == 0), stop=(j == tiles - 1))
                                mm.then_inc(y_done, 1)
                            if exists(n, -1):
                                pe.wait_ge(h_ready, n)
                                for j in range(tiles):
                                    mm = nc.tensor.transpose(bank_ht[0:F, P * j:P * j + P], H[:, v, F * j:F * j + F], ident[:])
                                mm.then_inc(ht_done, 1)

                        pipeline(pe, step)

                    @block.scalar
                    def _(act):
                        act.wait_ge(params_in, 16 * N_PARAMS)
                        act.wait_ge(ones_done, 1)
                        nc.scalar.activation(w_high[:], w_low[:].bitcast(F32), ACT.Copy).then_inc(high_ready, 1)

                        def step(n, r):
                            u, v = r % 2, 1 - r % 2
                            if exists(n, 2):
                                act.wait_ge(t_done, n + 3)
                                need(act, u_done, n - 1)
                                nc.scalar.activation(XH[:, (r + 2) % 4, :], bank_t[:, 0:P], ACT.Copy).then_inc(xh_ready, 1)
                            if layer == 1 and exists(n, 0):
                                act.wait_ge(g_done, n + 1)
                                need(act, us_ready, n - 1)
                                nc.scalar.activation(GS[:, u, :], bank_g[u][:, 0:W], ACT.Silu).then_inc(gs_ready, 1)
                            if exists(n, -2):
                                act.wait_ge(y_done, n - 1)
                                if exists(n, -6):
                                    act.wait_ge(y_out[(r + 2) % 4], ring(n - 6, (r + 2) % 4))
                                nc.scalar.activation(Y[:, (r + 2) % 4, :], bank_y[u][:, 0:D], ACT.Copy).then_inc(y_ready, 1)
                            if exists(n, -1):
                                act.wait_ge(ht_done, n)
                                need(act, y_done, n - 2)
                                nc.scalar.activation(HT[0:F, v, :, :], bank_ht[0:F, 0:tiles * P].rearrange("p (j k) -> p j k", j=tiles),
                                                     ACT.Copy).then_inc(ht_ready, 1)
                            if layer == 0 and exists(n, 0):
                                act.wait_ge(hp_ready, n + 1)
                                need(act, ht_done, n - 1)
                                nc.scalar.activation(H[:, u, :], HP[:, u, :], ACT.Silu).then_inc(h_ready, 1)

                        pipeline(act, step)

                    @block.vector
                    def _(dve):
                        dve.wait_ge(high_ready, 1)
                        nc.vector.tensor_tensor(w_low[:], w_low[:].bitcast(F32), w_high[:].bitcast(F32),
                                                ALU.subtract).then_inc(low_ready, 1)

                        def low_part(n, r):
                            if exists(n, 2):
                                dve.wait_ge(xh_ready, n + 3)
                                need(dve, u_done, n - 1)
                                nc.vector.tensor_tensor(XL[:, (r + 2) % 4, :], bank_t[:, 0:P], XH[:, (r + 2) % 4, :].bitcast(F32),
                                                        ALU.subtract).then_inc(xl_ready, 1)

                        def step(n, r):
                            u, v = r % 2, 1 - r % 2
                            if layer == 1 or not exists(n, 0):
                                low_part(n, r)
                            if exists(n, 0) and layer == 0:
                                e = dve.value_load(expert_of[0:1, bass.ds(n, 1)], min_val=0, max_val=EXPERTS - 1)
                                dve.wait_ge(g_done, n + 1)
                                need(dve, hp_ready, n - 1)
                                nc.vector.tensor_tensor(GS[:, u, :], bank_g[u][:, 0:W], bias[:, 0, e, :], ALU.add).then_inc(gs_ready, 1)
                                dve.wait_ge(u_done, n + 1)
                                nc.vector.tensor_tensor(US[:, u, :], bank_u[u][:, 0:W], bias[:, 1, e, :], ALU.add).then_inc(us_ready, 1)
                                low_part(n, r)
                                dve.wait_ge(us_ready, n + 1)
                                need(dve, h_ready, n - 1)
                                nc.vector.tensor_tensor(HP[:, u, :], GS[:, u, :], US[:, u, :], ALU.mult).then_inc(hp_ready, 1)
                            if exists(n, 0) and layer == 1:
                                dve.wait_ge(u_done, n + 1)
                                dve.wait_ge(gs_ready, n + 1)
                                need(dve, ht_done, n - 1)
                                nc.vector.tensor_tensor(H[:, u, :], bank_u[u][:, 0:W], GS[:, u, :], ALU.mult).then_inc(us_ready, 1)

                        pipeline(dve, step)

        def combine(layer):
            QUARTER = B // 4
            with ExitStack() as inner:
                R = inner.enter_context(nc.sbuf_tensor(f"R_C{layer}", [P, 2, B, D], F32))
                landed = [inner.enter_context(nc.semaphore(f"landed{i}_C{layer}")) for i in range(4)]
                first_done = inner.enter_context(nc.semaphore(f"first_done_C{layer}"))
                with nc.Block() as block:
                    @block.sync
                    def _(sp):
                        rows = results[0:TRASH].rearrange("(c b p) d -> p c b d", c=2, p=P)
                        for i in range(4):
                            for c in range(2):
                                part = slice(QUARTER * i, QUARTER * i + QUARTER)
                                sp.dma_start(R[:, c, part, :], rows[:, c, part, :]).then_inc(landed[i], 16)

                    @block.vector
                    def _(dve):
                        for i in range(4):
                            dve.wait_ge(landed[i], 32)
                            for c in range(2):
                                if c == 1:
                                    dve.wait_ge(first_done, QUARTER * (i + 1))
                                with dve.Fori(QUARTER * i, QUARTER * i + QUARTER) as b:
                                    ins = nc.vector.scalar_tensor_tensor(X[:, b, :], R[:, c, b, :], weight[:, c, bass.ds(b, 1)],
                                                                         X[:, b, :], ALU.mult, ALU.add)
                                    if c == 0:
                                        ins.then_inc(first_done, 1)

        def clear_semaphores():
            used = sorted(nc.released_uncleared_semaphores)
            with nc.Block() as block:
                @block.gpsimd
                def _(pool):
                    first = used[0]
                    for number, following in zip(used, used[1:] + [None]):
                        if following != number + 1:
                            pool.sem_clear(range(first, number + 1))
                            first = following

        def store():
            with ExitStack() as sems:
                stored = sems.enter_context(nc.semaphore("stored"))
                with nc.Block() as block:
                    @block.sync
                    def _(sp):
                        sp.dma_start(t["out"].rearrange("b p d -> p b d"), X[:]).then_inc(stored, 16)
                        sp.wait_ge(stored, 16)

        load_constants()
        for layer in range(2):
            layer_norm_stats(f"A{layer}")
            attention(layer)
            layer_norm_stats(f"F{layer}")
            route(layer)
            experts(layer)
            combine(layer)
            if layer == 0:
                clear_semaphores()
        store()


def _layouts(inputs):
    import numpy as np

    a = {k: np.asarray(v) for k, v in inputs.items()}
    out = {"x": a["x"], "ctx": a["ctx_1024"]}

    def heads_out(w):
        v = np.zeros((D, GROUPS, QUADS, SLOT), w.dtype)
        for part in range(3):
            v[..., HD * part:HD * part + HD] = w.T.reshape(D, GROUPS, QUADS, HD)
        return v.reshape(D, GROUPS, P)

    def heads_bias(b, one):
        v = np.zeros((QUADS, SLOT, GROUPS), b.dtype)
        for part in range(3):
            v[:, HD * part:HD * part + HD, :] = b.reshape(GROUPS, QUADS, HD).transpose(1, 2, 0)
        if one:
            v[:, ONES:ONES + 2, :] = 1
        return v.reshape(P, GROUPS)

    def low_rows(part):
        v = np.zeros((QUADS, SLOT, 1), np.float32)
        v[:, HD * part:HD * part + HD] = 1
        return v.reshape(P, 1)

    out["q_low"], out["k_low"] = low_rows(2), low_rows(1)
    for n in range(2):
        p = f"L{n}_xattn_"
        out[f"L{n}_WqP"] = heads_out(a[p + "Wq"])
        out[f"L{n}_WkP"] = heads_out(a[p + "Wk"])
        out[f"L{n}_WvT"] = a[p + "Wv"].T
        out[f"L{n}_WoT"] = a[p + "Wo"].T
        out[f"L{n}_bqP"] = heads_bias(a[p + "bq"], False)
        out[f"L{n}_bkP"] = heads_bias(a[p + "bk"], True)
        out[f"L{n}_bvB"] = np.broadcast_to(a[p + "bv"], (P, D))
        out[f"L{n}_boB"] = np.broadcast_to(a[p + "bo"], (P, D))
    out["L0_gateT"] = a["L0_ffn_gate_w"].T
    out["L1_gateT"] = a["L1_ffn_wg"].T
    out["L0_gateB"] = np.broadcast_to(a["L0_ffn_gate_b"], (P, EXPERTS))
    for n, g, u, dn, tiles in ((0, "L0_ffn_gp_w", "L0_ffn_up_w", "L0_ffn_down_w", 4),
                               (1, "L1_ffn_w1", "L1_ffn_w3", "L1_ffn_w2", 2)):
        F = a[g].shape[1] // tiles
        out[f"L{n}_gpT"] = a[g].transpose(2, 0, 1)
        out[f"L{n}_upT"] = a[u].transpose(2, 0, 1)
        dT = a[dn].transpose(2, 0, 1).reshape(tiles, F, EXPERTS, D).transpose(1, 2, 0, 3)
        if n == 0:
            full = np.zeros((F + 1, EXPERTS, tiles, D), dT.dtype)
            full[:F] = dT
            full[F, :, 0, :] = a["L0_ffn_down_b"]
            dT = full
        out[f"L{n}_downT"] = dT
    out["L0_biasB"] = np.broadcast_to(np.stack([a["L0_ffn_gp_b"], a["L0_ffn_up_b"]]), (P, 2, EXPERTS, a["L0_ffn_gp_b"].shape[1]))
    return {k: np.ascontiguousarray(v) for k, v in out.items()}


def kernel(**inputs):
    import numpy as _np
    import concourse.bacc as _bacc
    from concourse import mybir as _mybir
    from concourse.bass_utils import run_bass_kernel_spmd as _run

    nc = _bacc.Bacc("TRN2", target_bir_lowering=False, num_devices=1)
    arrays, tensors = {}, {}
    for name, a in _layouts(inputs).items():
        arrays[f"in_{name}"] = a
        tensors[name] = nc.dram_tensor(f"in_{name}", a.shape, _mybir.dt.from_np(a.dtype), kind="ExternalInput").ap()
    shape = inputs["x"].shape
    tensors["out"] = nc.dram_tensor("out_x", shape, F32, kind="ExternalOutput").ap()
    build_program(nc, tensors)
    r = _run(nc, [arrays], core_ids=[0])
    return r.results[0]["out_x"]
```

```python
from contextlib import ExitStack

import concourse.bass as bass
from concourse import mybir

F32 = mybir.dt.float32
F32R = mybir.dt.float32r
ALU = mybir.AluOpType
ACT = mybir.ActivationFunctionType
BF16 = mybir.dt.bfloat16
I32 = mybir.dt.int32
AX_X = mybir.AxisListType.X

P = 128
D = 128
HEADS = 16
HD = D // HEADS
QUADS = 4
GROUPS = HEADS // QUADS
SLOT = 32
ONES = 3 * HD
EXPERTS = 8
EPS = 1e-5


def need(engine, semaphore, count):
    if not isinstance(count, int) or count > 0:
        engine.wait_ge(semaphore, count)


def build_program(nc, t):
    B = t["x"].shape[0]
    NCH = B // 4
    TOKENS = B * P
    SUBTILES = 2 * B + EXPERTS
    TRASH = 2 * TOKENS
    ROUND = float(3 * 2 ** 22)

    with ExitStack() as ctx:
        def sb(name, shape):
            return ctx.enter_context(nc.sbuf_tensor(name, shape, F32))

        banks = [ctx.enter_context(nc.psum_tensor(f"bank{i}", [P, 512], F32)) for i in range(8)]

        X = sb("X", [P, B, D])
        weight = sb("weight", [P, 2, B])
        ident = sb("ident", [P, P])
        mean = sb("mean", [P, B])
        rstd = sb("rstd", [P, B])
        minus_half = sb("minus_half", [P, B])
        earlier = sb("earlier", [P, P])
        ones = sb("ones", [P, P])
        count = sb("count", [P, P])
        count_p = sb("count_p", [P, 1])
        index = ctx.enter_context(nc.sbuf_tensor("index", [P, 2, SUBTILES], I32))
        expert_of = ctx.enter_context(nc.sbuf_tensor("expert_of", [P, SUBTILES], I32))

        xn_rows = nc.dram_tensor("xn_rows", [TOKENS, D], F32, kind="Internal").ap()
        results = nc.dram_tensor("results", [TRASH + SUBTILES * P, D], F32, kind="Internal").ap()

        x_in = [ctx.enter_context(nc.semaphore(f"x_in{i}")) for i in range(4)]

        def load_constants():
            with ExitStack() as sems:
                zeroed = sems.enter_context(nc.semaphore("ident_zeroed"))
                count_i = sems.enter_context(nc.sbuf_tensor("count_i", [P, P], I32))
                count_pi = sems.enter_context(nc.sbuf_tensor("count_pi", [P, 1], I32))
                with nc.Block() as block:
                    @block.sync
                    def _(sp):
                        for i in range(4):
                            part = slice(B // 4 * i, B // 4 * i + B // 4)
                            sp.dma_start(X[:, part, :], t["x"].rearrange("b p d -> p b d")[:, part, :]).then_inc(x_in[i], 16)

                    @block.gpsimd
                    def _(pool):
                        nc.gpsimd.memset(minus_half[:], -0.5)
                        nc.gpsimd.memset(ident[:], 0.0).then_inc(zeroed, 1)
                        nc.gpsimd.memset(ones[:], 1.0).then_inc(zeroed, 1)
                        nc.gpsimd.iota(count_i[:], [[1, P]], base=0, channel_multiplier=0).then_inc(zeroed, 1)
                        nc.gpsimd.iota(count_pi[:], [[1, 1]], base=1, channel_multiplier=1).then_inc(zeroed, 1)
                        pool.wait_ge(zeroed, 4)
                        nc.gpsimd.affine_select(out=ident[:], in_=ident[:], compare_op=ALU.not_equal, fill=1.0,
                                                base=0, pattern=[[-1, P]], channel_multiplier=1)
                        nc.gpsimd.affine_select(out=earlier[:], in_=ones[:], compare_op=ALU.is_gt, fill=0.0,
                                                base=0, pattern=[[1, P]], channel_multiplier=-1)
                        nc.gpsimd.tensor_copy(count[:], count_i[:])
                        nc.gpsimd.tensor_copy(count_p[:], count_pi[:])

        def layer_norm(inner, tag):
            stats = inner.enter_context(nc.sbuf_tensor(f"stats_{tag}", [P, B, 6], F32))
            half = inner.enter_context(nc.sbuf_tensor(f"half_{tag}", [P, 3, B], F32))
            stats_done = inner.enter_context(nc.semaphore(f"stats_done_{tag}"))
            aggr_done = inner.enter_context(nc.semaphore(f"aggr_done_{tag}"))
            eps_done = inner.enter_context(nc.semaphore(f"eps_done_{tag}"))
            rstd_ready = inner.enter_context(nc.semaphore(f"rstd_ready_{tag}"))

            def on_vector(dve):
                def statistics(j):
                    for k in range(8):
                        ins = nc.vector.bn_stats(stats[:, 8 * j + k, :], X[:, 8 * j + k, :])
                    ins.then_inc(stats_done, 1)

                if tag == "A0":
                    for j in range(B // 8):
                        if j % (B // 32) == 0:
                            dve.wait_ge(x_in[j // (B // 32)], 16)
                        statistics(j)
                else:
                    with dve.Fori(0, B // 8) as j:
                        statistics(j)
                dve.wait_ge(stats_done, B // 8)
                V = nc.vector
                mean_e, mean_o, sq_e, sq_o = (stats[:, :, k] for k in (1, 4, 2, 5))
                V.tensor_tensor(half[:, 0, :], mean_e, mean_o, ALU.add).then_inc(aggr_done, 1)
                V.tensor_tensor(half[:, 1, :], mean_e, mean_o, ALU.subtract).then_inc(aggr_done, 1)
                V.tensor_tensor(half[:, 2, :], sq_e, sq_o, ALU.add).then_inc(aggr_done, 1)
                dve.wait_ge(aggr_done, 3)
                V.tensor_scalar(mean[:], half[:, 0, :], 0.5, None, ALU.mult).then_inc(aggr_done, 1)
                V.scalar_tensor_tensor(half[:, 1, :], half[:, 1, :], 0.25, half[:, 1, :], ALU.mult,
                                       ALU.mult).then_inc(aggr_done, 1)
                dve.wait_ge(aggr_done, 5)
                V.scalar_tensor_tensor(rstd[:], half[:, 2, :], 1.0 / D, half[:, 1, :], ALU.mult,
                                       ALU.add).then_inc(aggr_done, 1)

            def on_gpsimd(pool):
                pool.wait_ge(aggr_done, 6)
                nc.gpsimd.tensor_scalar(rstd[:], rstd[:], 1.0, EPS, ALU.mult, ALU.add).then_inc(eps_done, 1)
                pool.wait_ge(eps_done, 1)
                for c in range(NCH):
                    part = rstd[:, 4 * c:4 * c + 4]
                    nc.gpsimd.tensor_tensor(part, part, minus_half[:, 4 * c:4 * c + 4], ALU.pow).then_inc(rstd_ready, 1)

            return on_vector, on_gpsimd, rstd_ready

        def attention(layer, prefetch):
            tag = f"L{layer}"
            scale = (1.0 / D ** 0.5) if layer == 0 else HD ** -0.5
            with ExitStack() as inner:
                def isb(name, shape, dtype=F32):
                    return inner.enter_context(nc.sbuf_tensor(f"{name}_{tag}", shape, dtype))

                def sem(name):
                    return inner.enter_context(nc.semaphore(f"{name}_{tag}"))

                QB = isb("QB", [P, 2, GROUPS, QUADS, P], F32R)
                KB = isb("KB", [P, 2, GROUPS, QUADS, P], F32R)
                norm_on_vector, norm_on_gpsimd, rstd_ready = layer_norm(inner, f"A{layer}")
                wq = isb("wq", [D, GROUPS, P])
                wk = isb("wk", [D, GROUPS, P])
                wv = isb("wv", [D, D])
                wo = isb("wo", [D, D])
                bq = isb("bq", [P, GROUPS])
                bk = isb("bk", [P, GROUPS])
                q_low = isb("q_low", [P, 1])
                k_low = isb("k_low", [P, 1])
                bv = isb("bv", [P, D])
                bo = isb("bo", [P, D])
                C = isb("C", [P, 4, D])
                XN = isb("XN", [P, 2, D])
                XB = isb("XB", [P, 2, D])
                XCT = isb("XCT", [D, 2, 2, P])
                ZQ = isb("ZQ", [P, 2, GROUPS, P])
                ZK = isb("ZK", [P, 2, GROUPS, P])
                HQ = isb("HQ", [P, 2, GROUPS, P], F32R)
                HK = isb("HK", [P, 2, GROUPS, P], F32R)
                QS = isb("QS", [P, 4, GROUPS, P], F32R)
                KS = isb("KS", [P, 4, GROUPS, P], F32R)
                QA = isb("QA", [P, 2, GROUPS, P], F32R)
                VA = isb("VA", [P, 4, HEADS, SLOT])
                NM = isb("NM", [P, 2, GROUPS, P])
                MX = isb("MX", [P, 2, HEADS])
                E = isb("E", [P, GROUPS, QUADS, P])
                OS = isb("OS", [P, 2, GROUPS, P])
                RD = isb("RD", [P, 2, HEADS])
                ON = isb("ON", [P, 2, D])
                ONT = isb("ONT", [D, 2, P])

                bank_t, bank_q, bank_k, bank_o = banks[0], banks[1], banks[2], banks[7]
                bank_s, bank_st = banks[3:5], banks[5:7]

                params_in = sem("params_in")
                ctx_in = [sem("ctx_in0"), sem("ctx_in1")]
                kb_in = [sem("kb_in0"), sem("kb_in1")]
                qb_in = [sem("qb_in0"), sem("qb_in1")]
                fill_done = sem("fill_done")
                xn_ready, xb_ready = sem("xn_ready"), sem("xb_ready")
                t_done, xct_ready = sem("t_done"), sem("xct_ready")
                q_done, k_done, v_done = sem("q_done"), sem("k_done"), sem("v_done")
                zq_ready, zk_ready, hq_ready, hk_ready = sem("zq_ready"), sem("zk_ready"), sem("hq_ready"), sem("hk_ready")
                q_ready, k_ready, v_ready = sem("q_ready"), sem("k_ready"), sem("v_ready")
                s_done, max_done, nh_ready, nm_ready = sem("s_done"), sem("max_done"), sem("nh_ready"), sem("nm_ready")
                mt_done, qa_ready = sem("mt_done"), sem("qa_ready")
                st_done, exp_done, pv_done, os_ready = sem("st_done"), sem("exp_done"), sem("pv_done"), sem("os_ready")
                ot_done, rd_ready, on_ready = sem("ot_done"), sem("rd_ready"), sem("on_ready")
                ont_done, ont_ready = sem("ont_done"), sem("ont_ready")
                out_done, x_done = sem("out_done"), sem("x_done")
                N_PARAMS = 10

                def pipeline(engine, step):
                    for n in range(-2, 4):
                        step(n, n % 4)
                    with engine.Fori(0, (B - 8) // 4) as j:
                        for r in range(4):
                            step(4 * j + 4 + r, r)
                    for n in range(B - 4, B + 3):
                        step(n, n % 4)

                def exists(n, ahead):
                    return not isinstance(n, int) or 0 <= n + ahead < B

                def loads(n, p):
                    return (n - p) * 8 + 16

                def by_head(a):
                    return a.rearrange("p (i k) -> p i k", i=QUADS)

                with nc.Block() as block:
                    @block.sync
                    def _(sp):
                        context = t["ctx"].rearrange("b p d -> p b d")
                        for dst, src in ((wq, "WqP"), (wk, "WkP"), (wv, "WvT"), (wo, "WoT"),
                                         (bq, "bqP"), (bk, "bkP"), (bv, "bvB"), (bo, "boB")):
                            sp.dma_start(dst[:], t[f"L{layer}_{src}"]).then_inc(params_in, 16)
                        sp.dma_start(q_low[:], t["q_low"]).then_inc(params_in, 16)
                        sp.dma_start(k_low[:], t["k_low"]).then_inc(params_in, 16)
                        for i in range(2):
                            sp.dma_start(C[:, 2 * i:2 * i + 2, :], context[:, 2 * i:2 * i + 2, :]).then_inc(ctx_in[i], 16)
                        for destination, source, loaded in prefetch:
                            sp.dma_start(destination, source).then_inc(loaded, 16)
                        sp.wait_ge(fill_done, 5)

                        def spread(dst, src, p, landed):
                            for i in range(QUADS):
                                rows = slice(SLOT * i, SLOT * i + SLOT)
                                sp.dma_start(dst[rows, p, :, i, :].bitcast(F32), src[rows, :, :].bitcast(F32)).then_inc(landed[p], 16)

                        def step(n, r):
                            p, q = r % 2, 1 - r % 2
                            if exists(n, 1):
                                sp.wait_ge(k_ready, n + 2)
                                spread(KB, KS[:, (r + 1) % 4, :, :], q, kb_in)
                            if exists(n, -1):
                                sp.wait_ge(qa_ready, n)
                                spread(QB, QA[:, q, :, :], q, qb_in)
                            if exists(n, 0) and exists(n, 4) and p == 0:
                                sp.wait_ge(t_done, n + 2)
                                sp.dma_start(C[:, r:r + 2, :], context[:, bass.ds(n + 4, 2), :]).then_inc(ctx_in[r // 2], 16)

                        pipeline(sp, step)

                    @block.gpsimd
                    def _(pool):
                        nc.gpsimd.memset(VA[:], 0.0).then_inc(fill_done, 1)
                        nc.gpsimd.memset(NM[:], 0.0).then_inc(fill_done, 1)
                        pool.wait_ge(fill_done, 2)
                        nc.gpsimd.memset(VA[:, :, :, HD:HD + 1], 1.0).then_inc(fill_done, 1)
                        nc.gpsimd.memset(KB[:].bitcast(F32), 0.0).then_inc(fill_done, 1)
                        nc.gpsimd.memset(QB[:].bitcast(F32), 0.0).then_inc(fill_done, 1)
                        norm_on_gpsimd(pool)
                        pool.wait_ge(params_in, N_PARAMS * 16)

                        def step(n, r):
                            p, q = r % 2, 1 - r % 2
                            if exists(n, -2):
                                need(pool, x_done, n - 3)
                                nc.gpsimd.tensor_tensor(XB[:, p, :], X[:, n - 2, :], bo[:], ALU.add).then_inc(xb_ready, 1)
                            if exists(n, 2):
                                pool.wait_ge(zk_ready, n + 3)
                                need(pool, k_ready, n + 1)
                                nc.gpsimd.tensor_tensor(HK[:, p, :, :], ZK[:, p, :, :], k_low[:].unsqueeze(2).to_broadcast([P, GROUPS, P]),
                                                        ALU.mult).then_inc(hk_ready, 1)
                                pool.wait_ge(zq_ready, n + 3)
                                need(pool, q_ready, n + 1)
                                nc.gpsimd.tensor_tensor(HQ[:, p, :, :], ZQ[:, p, :, :], q_low[:].unsqueeze(2).to_broadcast([P, GROUPS, P]),
                                                        ALU.mult).then_inc(hq_ready, 1)

                        pipeline(pool, step)

                    @block.tensor
                    def _(pe):
                        pe.wait_ge(params_in, N_PARAMS * 16)
                        pe.wait_ge(fill_done, 5)

                        def project(bank, w, x):
                            for g in range(GROUPS):
                                mm = nc.tensor.matmul(bank[:, P * g:P * g + P], w[:, g, :], x, start=True, stop=True)
                            return mm

                        def scores(n, r, g):
                            if g == 0:
                                pe.wait_ge(q_ready, n + 1)
                                pe.wait_ge(kb_in[r % 2], 4 * loads(n, r % 2))
                            need(pe, max_done, 4 * n + g - 1)
                            nc.tensor.matmul(bank_s[g % 2][:], QS[:, r, g, :], KB[:, r % 2, g, :, :],
                                             start=True, stop=True).then_inc(s_done, 1)

                        def transposed_scores(m, r, g):
                            if g == 0:
                                pe.wait_ge(qb_in[r % 2], 4 * loads(m, r % 2))
                            need(pe, exp_done, 4 * m + g - 1)
                            nc.tensor.matmul(bank_st[g % 2][:], KS[:, (r + 2) % 4, g, :], QB[:, r % 2, g, :, :],
                                             start=True, stop=True).then_inc(st_done, 1)

                        def weigh(m, r, g):
                            pe.wait_ge(exp_done, 4 * m + g + 1)
                            if g == 0:
                                need(pe, os_ready, m)
                            for i in range(QUADS):
                                mm = nc.tensor.matmul(bank_o[SLOT * i:SLOT * i + SLOT, P * g:P * g + P],
                                                      VA[:, (r + 2) % 4, QUADS * g + i, :], E[:, g, i, :],
                                                      start=True, stop=True)
                            if g == GROUPS - 1:
                                mm.then_inc(pv_done, 1)

                        def step(n, r):
                            p, q = r % 2, 1 - r % 2
                            mid, back, tail = exists(n, 0), exists(n, -2), exists(n, -3)
                            if mid:
                                scores(n, r, 0)
                                scores(n, r, 1)
                            if exists(n, 1):
                                pe.wait_ge(xct_ready, n + 2)
                                need(pe, x_done, n - 3)
                                nc.tensor.matmul(bank_t[:, 0:P], XCT[:, q, 1, :], wv[:],
                                                 start=True, stop=True).then_inc(v_done, 1)
                            if exists(n, -1):
                                pe.wait_ge(nm_ready, n)
                                if exists(n, 1):
                                    pe.wait_ge(zq_ready, n + 2)
                                for g in range(GROUPS):
                                    mm = nc.tensor.transpose(bank_q[:, P * g:P * g + P], NM[:, q, g, :], ident[:])
                                mm.then_inc(mt_done, 1)
                            if back:
                                transposed_scores(n - 2, r, 0)
                            if exists(n, 2):
                                pe.wait_ge(xn_ready, n + 3)
                                s4 = (r + 2) % 4
                                pe.wait_ge(ctx_in[s4 // 2], (n + 2 - s4) * 4 + 16)
                                if exists(n, 1):
                                    pe.wait_ge(v_ready, n + 2)
                                nc.tensor.transpose(bank_t[:, 0:P], XN[:, p, :], ident[:])
                                nc.tensor.transpose(bank_t[:, P:2 * P], C[:, s4, :], ident[:]).then_inc(t_done, 1)
                            if tail:
                                pe.wait_ge(os_ready, n - 2)
                                if exists(n, 1):
                                    pe.wait_ge(zk_ready, n + 2)
                                for g in range(GROUPS):
                                    mm = nc.tensor.transpose(bank_k[:, P * g:P * g + P], OS[:, q, g, :], ident[:])
                                mm.then_inc(ot_done, 1)
                            if back:
                                transposed_scores(n - 2, r, 1)
                            if mid:
                                scores(n, r, 2)
                            if back:
                                transposed_scores(n - 2, r, 2)
                                weigh(n - 2, r, 0)
                            if tail:
                                pe.wait_ge(on_ready, n - 2)
                                if exists(n, 2):
                                    pe.wait_ge(xct_ready, n + 3)
                                elif exists(n, 1):
                                    pe.wait_ge(v_ready, n + 2)
                                nc.tensor.transpose(bank_t[:, 0:P], ON[:, q, :], ident[:]).then_inc(ont_done, 1)
                            if exists(n, 2):
                                pe.wait_ge(xct_ready, n + 3)
                                if not tail and exists(n, 1):
                                    pe.wait_ge(zk_ready, n + 2)
                                project(bank_k, wk, XCT[:, p, 1, :]).then_inc(k_done, 1)
                            if mid:
                                scores(n, r, 3)
                            if back:
                                transposed_scores(n - 2, r, 3)
                                weigh(n - 2, r, 1)
                            if tail:
                                pe.wait_ge(ont_ready, n - 2)
                                nc.tensor.matmul(bank_t[:, 0:P], ONT[:, q, :], wo[:],
                                                 start=True, stop=True).then_inc(out_done, 1)
                            if back:
                                weigh(n - 2, r, 2)
                            if exists(n, 2):
                                need(pe, qa_ready, n)
                                if not exists(n, -1) and exists(n, 1):
                                    pe.wait_ge(zq_ready, n + 2)
                                project(bank_q, wq, XCT[:, p, 0, :]).then_inc(q_done, 1)
                            if back:
                                weigh(n - 2, r, 3)

                        pipeline(pe, step)

                    @block.scalar
                    def _(act):
                        act.wait_ge(params_in, N_PARAMS * 16)

                        def exponentials(m, g):
                            act.wait_ge(st_done, 4 * m + g + 1)
                            if g == 0:
                                need(act, pv_done, m)
                            nc.scalar.activation(E[:, g, :, :], by_head(bank_st[g % 2][:]), ACT.Exp,
                                                 scale=scale).then_inc(exp_done, 1)

                        def bias_add(m, u, bank, Z, b, done, ready, used):
                            act.wait_ge(done, m + 1)
                            need(act, used, m - 1)
                            for g in range(GROUPS):
                                ins = nc.scalar.activation(Z[:, u, g, :], bank[:, P * g:P * g + P], ACT.Identity,
                                                           bias=b[:, g:g + 1])
                            ins.then_inc(ready, 1)

                        def step(n, r):
                            p, q = r % 2, 1 - r % 2
                            if exists(n, -2):
                                exponentials(n - 2, 0)
                            if exists(n, 2):
                                act.wait_ge(t_done, n + 3)
                                need(act, v_done, n + 1)
                                nc.scalar.activation(XCT[:, p, :, :], bank_t[:, 0:2 * P].rearrange("p (a b) -> p a b", a=2),
                                                     ACT.Copy).then_inc(xct_ready, 1)
                            if exists(n, -2):
                                exponentials(n - 2, 1)
                                exponentials(n - 2, 2)
                            if exists(n, -3):
                                act.wait_ge(ont_done, n - 2)
                                need(act, out_done, n - 4)
                                nc.scalar.activation(ONT[:, q, :], bank_t[:, 0:P], ACT.Copy).then_inc(ont_ready, 1)
                            if exists(n, 2):
                                bias_add(n + 2, p, bank_k, ZK, bk, k_done, zk_ready, k_ready)
                            if exists(n, -2):
                                exponentials(n - 2, 3)
                            if exists(n, 2):
                                bias_add(n + 2, p, bank_q, ZQ, bq, q_done, zq_ready, q_ready)
                            if exists(n, -2):
                                act.wait_ge(pv_done, n - 1)
                                need(act, ot_done, n - 3)
                                nc.scalar.activation(OS[:, p, :, :], bank_o[:].rearrange("p (g k) -> p g k", g=GROUPS),
                                                     ACT.Copy).then_inc(os_ready, 1)

                        pipeline(act, step)

                    @block.vector
                    def _(dve):
                        norm_on_vector(dve)
                        dve.wait_ge(params_in, N_PARAMS * 16)
                        dve.wait_ge(fill_done, 5)

                        def maximum(n, p, g):
                            dve.wait_ge(s_done, 4 * n + g + 1)
                            nc.vector.tensor_reduce(MX[:, p, QUADS * g:QUADS * g + QUADS], by_head(bank_s[g % 2][:]),
                                                    AX_X, ALU.max).then_inc(max_done, 1)

                        def step(n, r):
                            p, q = r % 2, 1 - r % 2
                            mid = exists(n, 0)
                            if exists(n, 2):
                                need(dve, t_done, n + 1)
                                if isinstance(n, int) and n in (-2, 2):
                                    dve.wait_ge(rstd_ready, 1 if n == -2 else NCH)
                                nc.vector.tensor_scalar(XN[:, p, :], X[:, n + 2, :], mean[:, bass.ds(n + 2, 1)],
                                                        rstd[:, bass.ds(n + 2, 1)], ALU.subtract,
                                                        ALU.mult).then_inc(xn_ready, 1)
                            if exists(n, 1):
                                need(dve, pv_done, n - 2)
                                dve.wait_ge(hk_ready, n + 2)
                                nc.vector.tensor_tensor(KS[:, (r + 1) % 4, :, :], ZK[:, q, :, :], HK[:, q, :, :].bitcast(F32),
                                                        ALU.subtract).then_inc(k_ready, 1)
                            if mid:
                                maximum(n, p, 0)
                            if exists(n, 1):
                                dve.wait_ge(v_done, n + 2)
                                nc.vector.tensor_tensor(VA[:, (r + 1) % 4, :, 0:HD], bank_t[:, 0:P].rearrange("p (h d) -> p h d", h=HEADS),
                                                        bv[:].rearrange("p (h d) -> p h d", h=HEADS),
                                                        ALU.add).then_inc(v_ready, 1)
                            if exists(n, -1):
                                dve.wait_ge(mt_done, n)
                                if exists(n, -3):
                                    dve.wait_ge(qb_in[q], 4 * loads(n - 3, q))
                                nc.vector.tensor_tensor(QA[:, q, :, :], bank_q[:].rearrange("p (g k) -> p g k", g=GROUPS),
                                                        QS[:, (r + 3) % 4, :, :].bitcast(F32), ALU.add).then_inc(qa_ready, 1)
                            if exists(n, -3):
                                dve.wait_ge(ot_done, n - 2)
                                outs = bank_k[:].rearrange("p (h c) -> p h c", c=SLOT)
                                nc.vector.reciprocal(RD[:, q, :].rearrange("p (h o) -> p h o", o=1),
                                                     outs[:, :, HD:HD + 1]).then_inc(rd_ready, 1)
                            if exists(n, -3):
                                dve.wait_ge(rd_ready, n - 2)
                                need(dve, ont_done, n - 4)
                                nc.vector.tensor_tensor(ON[:, q, :].rearrange("p (h d) -> p h d", h=HEADS),
                                                        outs[:, :, 0:HD],
                                                        RD[:, q, :].unsqueeze(2).to_broadcast([P, HEADS, HD]),
                                                        ALU.mult).then_inc(on_ready, 1)
                            if mid:
                                maximum(n, p, 1)
                                maximum(n, p, 2)
                            if exists(n, 1):
                                dve.wait_ge(hq_ready, n + 2)
                                nc.vector.tensor_tensor(QS[:, (r + 1) % 4, :, :], ZQ[:, q, :, :], HQ[:, q, :, :].bitcast(F32),
                                                        ALU.subtract).then_inc(q_ready, 1)
                            if mid:
                                maximum(n, p, 3)
                                dve.wait_ge(max_done, 4 * n + 4)
                                maxima = MX[:, p, :].rearrange("p (g i) -> p g i", g=GROUPS)
                                high = NM[:, p, :, ONES:P:SLOT]
                                nc.vector.tensor_scalar(high.bitcast(F32R), maxima, -1.0, None, ALU.mult).then_inc(nh_ready, 1)
                            if exists(n, -3):
                                dve.wait_ge(out_done, n - 2)
                                dve.wait_ge(xb_ready, n - 2)
                                nc.vector.tensor_tensor(X[:, n - 3, :], bank_t[:, 0:P], XB[:, q, :],
                                                        ALU.add).then_inc(x_done, 1)
                            if mid:
                                dve.wait_ge(nh_ready, n + 1)
                                nc.vector.scalar_tensor_tensor(NM[:, p, :, ONES + 1:P:SLOT].bitcast(F32R), maxima, -1.0,
                                                               high, ALU.mult, ALU.subtract).then_inc(nm_ready, 1)

                        pipeline(dve, step)

        def route(layer, gate, gate_b, w_high, w_low, dw, bias, gate_in, gu_in, params_read, low_ready):
            tag = f"R{layer}"
            with ExitStack() as inner:
                def isb(name, shape, dtype=F32):
                    return inner.enter_context(nc.sbuf_tensor(f"{name}_{tag}", shape, dtype))

                def sem(name):
                    return inner.enter_context(nc.semaphore(f"{name}_{tag}"))

                norm_on_vector, norm_on_gpsimd, rstd_ready = layer_norm(inner, f"F{layer}")
                XN = isb("XN", [P, 4, 4, D])
                XT = isb("XT", [D, B, P])
                LG = isb("LG", [P, B, EXPERTS])
                PR = isb("PR", [P, B, EXPERTS])
                T1 = isb("T1", [P, B, EXPERTS])
                T2 = isb("T2", [P, B, EXPERTS])
                T3 = isb("T3", [P, B, EXPERTS])
                R1 = isb("R1", [P, B])
                V1 = isb("V1", [P, B])
                V2 = isb("V2", [P, B])
                KEEP = isb("KEEP", [P, B, EXPERTS])
                KEEPB = isb("KEEPB", [P, EXPERTS, B])
                TOT = isb("TOT", [P, EXPERTS, B])
                BEFORE = isb("BEFORE", [P, EXPERTS, B])
                OVER = isb("OVER", [P, EXPERTS, B])
                EDGE = isb("EDGE", [P, B])
                tiles_of = isb("tiles_of", [P, EXPERTS])
                tiles_to = isb("tiles_to", [P, EXPERTS])
                SLOT_OF = isb("SLOT_OF", [P, 2 * B])
                HI = isb("HI", [P, 2 * B])
                LO = isb("LO", [P, 2 * B])
                AT_LO = isb("AT_LO", [P, 2 * B, P], BF16)
                AT_HI = isb("AT_HI", [P, 2 * B, SUBTILES], BF16)
                WHO = isb("WHO", [P, 2 * B, 2, SUBTILES], BF16)
                IDS = isb("IDS", [P, 2, SUBTILES])
                UNUSED = isb("UNUSED", [P, SUBTILES])
                ROW = isb("ROW", [P, 2, SUBTILES])
                PASTEND = isb("PASTEND", [P, SUBTILES])
                PAST = isb("PAST", [P, SUBTILES, EXPERTS - 1])
                bank_t, bank_l, bank_r, bank_n, bank_i = banks[0:2], banks[2], banks[3], banks[4], banks[5]
                xn_ready, t_done, xt_ready = sem("xn_ready"), sem("t_done"), sem("xt_ready")
                lg_done, chain, exp_in, exp_out = sem("lg_done"), sem("chain"), sem("exp_in"), sem("exp_out")
                keep_ready, picked, counted, placed = sem("keep_ready"), sem("picked"), sem("counted"), sem("placed")
                rows_out = [sem(f"rows_out{i}") for i in range(4)]
                past_part, high_ready = sem("past_part"), sem("high_ready")
                lo_ready, hi_ready, token_ready, batch_ready, ids_done = (sem("lo_ready"), sem("hi_ready"),
                                                                     sem("token_ready"), sem("batch_ready"), sem("ids_done"))

                with nc.Block() as block:
                    @block.sync
                    def _(sp):
                        rows = xn_rows.rearrange("(b p) d -> p b d", p=P)

                        for c in range(NCH):
                            sp.wait_ge(xn_ready, c + 1)
                            sp.dma_start(rows[:, 4 * c:4 * c + 4, :], XN[:, c % 4, :, :]).then_inc(rows_out[c % 4], 16)
                        if layer == 0:
                            sp.dma_start(bias[:], t["L0_biasB"]).then_inc(params_read, 16)
                        for u in range(4):
                            sp.wait_ge(rows_out[u], 16 * NCH // 4)

                    @block.gpsimd
                    def _(pool):
                        norm_on_gpsimd(pool)
                        nc.gpsimd.memset(KEEP[:, :, 1:EXPERTS], 1.0)
                        nc.gpsimd.memset(KEEP[:, :, 0:1], 0.0).then_inc(keep_ready, 1)
                        nc.gpsimd.memset(KEEPB[:, :, 1:B], 1.0)
                        nc.gpsimd.memset(KEEPB[:, :, 0:1], 0.0)
                        nc.gpsimd.tensor_scalar(PASTEND[:], count[:, 0:SUBTILES], float(P), float(TRASH), ALU.mult,
                                                ALU.add).then_inc(past_part, 1)
                        pool.wait_ge(past_part, 1)
                        nc.gpsimd.tensor_tensor(PASTEND[:], PASTEND[:], count_p[:].to_broadcast([P, SUBTILES]), ALU.add)
                        nc.gpsimd.tensor_scalar(EDGE[:], count[:, 0:B], float(P), None, ALU.mult).then_inc(keep_ready, 1)
                        pool.wait_ge(high_ready, 1)

                        def low_part(i):
                            nc.gpsimd.tensor_tensor(w_low[:, i, :, :], w_low[:, i, :, :].bitcast(F32), w_high[:, i, :, :].bitcast(F32),
                                                    ALU.subtract).then_inc(low_ready, 1)

                        low_part(0)
                        for half in range(2):
                            part = slice(B * half, B * half + B)
                            pool.wait_ge(hi_ready, half + 1)
                            nc.gpsimd.tensor_tensor(WHO[:, part, 1, :], AT_HI[:, part, :],
                                                    count[:, part].unsqueeze(2).to_broadcast([P, B, SUBTILES]),
                                                    ALU.mult).then_inc(batch_ready, 1)
                        low_part(1)

                    @block.tensor
                    def _(pe):
                        pe.wait_ge(gate_in, 32)

                        for c in range(NCH + 1):
                            if c < NCH:
                                pe.wait_ge(xn_ready, c + 1)
                                need(pe, xt_ready, c - 1)
                                for k in range(4):
                                    mm = nc.tensor.transpose(bank_t[c % 2][:, P * k:P * k + P], XN[:, c % 4, k, :], ident[:])
                                mm.then_inc(t_done, 1)
                            if c >= 1:
                                pe.wait_ge(xt_ready, c)
                                for b in range(4 * c - 4, 4 * c):
                                    mm = nc.tensor.matmul(bank_l[:, EXPERTS * b:EXPERTS * b + EXPERTS], XT[:, b, :], gate[:],
                                                          start=True, stop=True)
                        mm.then_inc(lg_done, 1)
                        pe.wait_ge(picked, 1)
                        chosen = T2[:].rearrange("p b e -> p (b e)")
                        nc.tensor.matmul(bank_r[:, 0:B * EXPERTS], earlier[:], chosen, start=True, stop=True)
                        nc.tensor.matmul(bank_n[:, 0:B * EXPERTS], ones[:], chosen, start=True, stop=True).then_inc(counted, 1)
                        for k in range(2 * B):
                            if k % B == 0:
                                pe.wait_ge(lo_ready, k // B + 1)
                                pe.wait_ge(token_ready, k // B + 1)
                                pe.wait_ge(batch_ready, k // B + 1)
                            mm = nc.tensor.matmul(bank_i[:, 0:2 * SUBTILES], AT_LO[:, k, :], WHO[:, k, :, :],
                                                  start=(k == 0), stop=(k == 2 * B - 1))
                        mm.then_inc(ids_done, 1)

                    @block.scalar
                    def _(act):
                        for c in range(NCH):
                            act.wait_ge(t_done, c + 1)
                            nc.scalar.activation(XT[:, 4 * c:4 * c + 4, :], bank_t[c % 2][:].rearrange("p (k c) -> p k c", k=4),
                                                 ACT.Copy).then_inc(xt_ready, 1)
                        act.wait_ge(exp_in, 1)
                        nc.scalar.activation(PR[:], LG[:], ACT.Exp).then_inc(exp_out, 1)
                        act.wait_ge(gu_in, 32)
                        nc.scalar.activation(w_high[:], w_low[:].bitcast(F32), ACT.Copy).then_inc(high_ready, 1)
                        for half in range(2):
                            part = slice(B * half, B * half + B)
                            act.wait_ge(hi_ready, half + 1)
                            nc.scalar.activation(WHO[:, part, 0, :], AT_HI[:, part, :], ACT.Copy,
                                                 scale=count_p[:]).then_inc(token_ready, 1)

                    @block.vector
                    def _(dve):
                        norm_on_vector(dve)
                        for c in range(NCH):
                            dve.wait_ge(rstd_ready, c + 1)
                            if c >= 4:
                                dve.wait_ge(t_done, c - 3)
                                dve.wait_ge(rows_out[c % 4], 16 * (c // 4))
                            for k in range(4):
                                b = 4 * c + k
                                ins = nc.vector.tensor_scalar(XN[:, c % 4, k, :], X[:, b, :], mean[:, b:b + 1], rstd[:, b:b + 1],
                                                              ALU.subtract, ALU.mult)
                            ins.then_inc(xn_ready, 1)

                        chained = [0]

                        def then(ins):
                            chained[0] += 1
                            ins.then_inc(chain, 1)
                            dve.wait_ge(chain, chained[0])

                        V = nc.vector

                        def wide(a):
                            return a[:].unsqueeze(2).to_broadcast([P, B, EXPERTS])

                        dve.wait_ge(gate_in, 32)
                        dve.wait_ge(keep_ready, 2)
                        dve.wait_ge(lg_done, 1)
                        logits = bank_l[:, 0:B * EXPERTS].rearrange("p (b e) -> p b e", e=EXPERTS)
                        if layer == 0:
                            then(V.tensor_tensor(T1[:], logits, gate_b[:].unsqueeze(1).to_broadcast([P, B, EXPERTS]), ALU.add))
                        else:
                            then(V.tensor_copy(T1[:], logits))
                        then(V.tensor_reduce(R1[:], T1[:], AX_X, ALU.max))
                        V.tensor_tensor(LG[:], T1[:], wide(R1), ALU.subtract).then_inc(exp_in, 1)
                        dve.wait_ge(exp_out, 1)
                        then(V.tensor_reduce(R1[:], PR[:], AX_X, ALU.add))
                        then(V.reciprocal(V1[:], R1[:]))
                        then(V.tensor_tensor(T1[:], PR[:], wide(V1), ALU.mult))
                        then(V.tensor_reduce(V1[:], T1[:], AX_X, ALU.max))
                        then(V.tensor_tensor(T2[:], T1[:], wide(V1), ALU.is_equal))
                        then(V.tensor_tensor_scan(T3[:].rearrange("p b e -> p (b e)"), KEEP[:].rearrange("p b e -> p (b e)"),
                                                  T2[:].rearrange("p b e -> p (b e)"), 0.0, ALU.mult, ALU.add))
                        then(V.scalar_tensor_tensor(T2[:], T3[:], 1.0, T2[:], ALU.is_equal, ALU.mult))
                        then(V.scalar_tensor_tensor(PR[:], T2[:], -2.0, T1[:], ALU.mult, ALU.add))
                        then(V.tensor_reduce(V2[:], PR[:], AX_X, ALU.max))
                        then(V.tensor_tensor(LG[:], PR[:], wide(V2), ALU.is_equal))
                        then(V.tensor_tensor_scan(T3[:].rearrange("p b e -> p (b e)"), KEEP[:].rearrange("p b e -> p (b e)"),
                                                  LG[:].rearrange("p b e -> p (b e)"), 0.0, ALU.mult, ALU.add))
                        then(V.scalar_tensor_tensor(LG[:], T3[:], 1.0, LG[:], ALU.is_equal, ALU.mult))
                        then(V.tensor_copy(PR[:], T2[:]))
                        V.tensor_tensor(T2[:], T2[:], LG[:], ALU.add).then_inc(picked, 1)
                        then(V.tensor_tensor(R1[:], V1[:], V2[:], ALU.add))
                        if layer == 0:
                            then(V.tensor_scalar(R1[:], R1[:], 1e-20, None, ALU.add))
                        then(V.reciprocal(R1[:], R1[:]))
                        then(V.tensor_tensor(weight[:, 0, :], V1[:], R1[:], ALU.mult))
                        then(V.tensor_tensor(weight[:, 1, :], V2[:], R1[:], ALU.mult))

                        def flat(a):
                            return a[:].rearrange("p e b -> p (e b)")

                        def by_expert(bank):
                            return bank[:, 0:B * EXPERTS].rearrange("p (b e) -> p e b", e=EXPERTS)

                        def over_batches(a):
                            return a[:].unsqueeze(2).to_broadcast([P, EXPERTS, B])

                        dve.wait_ge(counted, 1)
                        then(V.tensor_copy(TOT[:], by_expert(bank_n)))
                        then(V.tensor_tensor_scan(flat(BEFORE), flat(KEEPB), flat(TOT), 0.0, ALU.mult, ALU.add))
                        then(V.tensor_tensor(OVER[:], BEFORE[:, :, B - 1:B].to_broadcast([P, EXPERTS, B]),
                                             EDGE[:].unsqueeze(1).to_broadcast([P, EXPERTS, B]), ALU.is_gt))
                        then(V.tensor_reduce(tiles_of[:], OVER[:], AX_X, ALU.add))
                        then(V.tensor_tensor_scan(tiles_to[:], ones[:, 0:EXPERTS], tiles_of[:], 0.0, ALU.mult, ALU.add))
                        then(V.tensor_tensor(BEFORE[:], BEFORE[:], TOT[:], ALU.subtract))
                        then(V.tensor_tensor(tiles_of[:], tiles_to[:], tiles_of[:], ALU.subtract))
                        then(V.scalar_tensor_tensor(BEFORE[:], over_batches(tiles_of), float(P), BEFORE[:], ALU.mult, ALU.add))
                        then(V.tensor_tensor(BEFORE[:], BEFORE[:], by_expert(bank_r), ALU.add))
                        slots = BEFORE[:].rearrange("p e b -> p b e")
                        then(V.tensor_tensor(PR[:], PR[:], slots, ALU.mult))
                        then(V.tensor_tensor(LG[:], LG[:], slots, ALU.mult))
                        then(V.tensor_reduce(SLOT_OF[:, 0:B], PR[:], AX_X, ALU.add))
                        then(V.tensor_reduce(SLOT_OF[:, B:2 * B], LG[:], AX_X, ALU.add))
                        then(V.tensor_scalar(HI[:], SLOT_OF[:], 1.0 / P, -(P - 1) / (2.0 * P), ALU.mult, ALU.add))
                        then(V.tensor_scalar(HI[:], HI[:], ROUND, None, ALU.add))
                        then(V.tensor_scalar(HI[:], HI[:], ROUND, None, ALU.subtract))
                        V.scalar_tensor_tensor(LO[:], HI[:], -float(P), SLOT_OF[:], ALU.mult, ALU.add).then_inc(placed, 1)
                        dve.wait_ge(placed, 1)
                        for half in range(2):
                            part = slice(B * half, B * half + B)
                            V.tensor_tensor(AT_HI[:, part, :], count[:, 0:SUBTILES].unsqueeze(1).to_broadcast([P, B, SUBTILES]),
                                            HI[:, part].unsqueeze(2).to_broadcast([P, B, SUBTILES]), ALU.is_equal).then_inc(hi_ready, 1)
                            V.tensor_tensor(AT_LO[:, part, :], count[:].unsqueeze(1).to_broadcast([P, B, P]),
                                            LO[:, part].unsqueeze(2).to_broadcast([P, B, P]), ALU.is_equal).then_inc(lo_ready, 1)
                        then(V.tensor_tensor(PAST[:], count[:, 0:SUBTILES].unsqueeze(2).to_broadcast([P, SUBTILES, EXPERTS - 1]),
                                             tiles_to[:, 0:EXPERTS - 1].unsqueeze(1).to_broadcast([P, SUBTILES, EXPERTS - 1]),
                                             ALU.is_ge))
                        then(V.tensor_reduce(UNUSED[:], PAST[:], AX_X, ALU.add))
                        then(V.tensor_copy(expert_of[:], UNUSED[:]))
                        dve.wait_ge(ids_done, 1)
                        then(V.tensor_copy(IDS[:], bank_i[:, 0:2 * SUBTILES].rearrange("p (a k) -> p a k", a=2)))
                        then(V.tensor_scalar(UNUSED[:], IDS[:, 0, :], 0.5, None, ALU.is_lt))
                        then(V.scalar_tensor_tensor(IDS[:, 0, :], IDS[:, 1, :], float(P), IDS[:, 0, :], ALU.mult, ALU.add))
                        then(V.tensor_tensor(ROW[:, 1, :], UNUSED[:], PASTEND[:], ALU.mult))
                        then(V.scalar_tensor_tensor(ROW[:, 1, :], IDS[:, 0, :], 1.0, ROW[:, 1, :], ALU.subtract, ALU.add))
                        then(V.tensor_scalar(ROW[:, 0, :], IDS[:, 0, :], TOKENS + 0.5, -float(TOKENS), ALU.is_ge, ALU.mult))
                        then(V.tensor_tensor(ROW[:, 0, :], ROW[:, 0, :], IDS[:, 0, :], ALU.add))
                        then(V.tensor_scalar(UNUSED[:], UNUSED[:], count_p[:], -1.0, ALU.mult, ALU.add))
                        then(V.tensor_tensor(ROW[:, 0, :], ROW[:, 0, :], UNUSED[:], ALU.add))
                        then(V.tensor_copy(index[:], ROW[:]))

        def experts(layer, gate, gate_b, w_high, w_low, dw, bias, gate_in, gu_in, params_read, low_ready):
            tag = f"F{layer}"
            tiles, F = hidden(layer)
            W = tiles * F
            KD = F + 1 if layer == 0 else F
            with ExitStack() as inner:
                def isb(name, shape, dtype=F32):
                    return inner.enter_context(nc.sbuf_tensor(f"{name}_{tag}", shape, dtype))

                def sem(name):
                    return inner.enter_context(nc.semaphore(f"{name}_{tag}"))

                XG = isb("XG", [P, 4, D])
                XH = isb("XH", [D, 4, P], F32R)
                XL = isb("XL", [D, 4, P], F32R)
                GS = isb("GS", [P, 2, W])
                US = isb("US", [P, 2, W])
                H = isb("H", [P, 2, W])
                HT = isb("HT", [P, 2, tiles, P])
                Y = isb("Y", [P, 4, D])
                if layer == 0:
                    HP = isb("HP", [P, 2, W])
                ones_done = sem("ones_done")
                xg_in = [sem(f"xg_in{i}") for i in range(4)]
                y_out = [sem(f"y_out{i}") for i in range(4)]
                t_done, xh_ready, xl_ready = sem("t_done"), sem("xh_ready"), sem("xl_ready")
                g_done, u_done, gs_ready, us_ready = sem("g_done"), sem("u_done"), sem("gs_ready"), sem("us_ready")
                hp_ready, h_ready = sem("hp_ready"), sem("h_ready")
                if layer == 1:
                    h_ready = us_ready
                ht_done, ht_ready, y_done, y_ready = sem("ht_done"), sem("ht_ready"), sem("y_done"), sem("y_ready")
                bank_t, bank_ht = banks[0], banks[1]
                bank_g, bank_u, bank_y = banks[2:4], banks[4:6], banks[6:8]
                N_PARAMS = 2 if layer == 0 else 1
                S = SUBTILES

                def pipeline(engine, step):
                    for n in range(-2, 8):
                        step(n, n % 4)
                    with engine.Fori(0, (S - 12) // 4) as j:
                        for r in range(4):
                            step(4 * j + 8 + r, r)
                    for n in range(S - 4, S + 2):
                        step(n, n % 4)

                def exists(n, ahead):
                    return not isinstance(n, int) or 0 <= n + ahead < S

                def ring(n, r):
                    return (n - r) * 4 + 16

                with nc.Block() as block:
                    @block.gpsimd
                    def _(pool):
                        nc.gpsimd.memset(HT[:], 1.0).then_inc(ones_done, 1)

                        def gather(n):
                            need(pool, t_done, n - 3)
                            pool.indirect_dma_start(XG[:, n % 4, :], None, xn_rows,
                                                    bass.IndirectOffsetOnAxis(index[:, 0, n:n + 1], 0)).then_inc(xg_in[n % 4], 16)

                        def scatter(n):
                            pool.wait_ge(y_ready, n + 1)
                            pool.indirect_dma_start(results, bass.IndirectOffsetOnAxis(index[:, 1, n:n + 1], 0),
                                                    Y[:, n % 4, :], None).then_inc(y_out[n % 4], 16)

                        for n in range(S + 3):
                            if n < S:
                                gather(n)
                            if n >= 3 + 3:
                                scatter(n - 6)
                        for n in range(S - 3, S):
                            scatter(n)
                        for i in range(4):
                            pool.wait_ge(y_out[i], 16 * S // 4)

                    @block.tensor
                    def _(pe):
                        pe.wait_ge(params_read, 16 * N_PARAMS)
                        pe.wait_ge(low_ready, 2)
                        pe.wait_ge(ones_done, 1)

                        held = {}

                        def expert(n):
                            return pe.value_load(expert_of[0:1, bass.ds(n, 1)], min_val=0, max_val=EXPERTS - 1)

                        def step(n, r):
                            u, v = r % 2, 1 - r % 2
                            if exists(n, 0):
                                e = held[r] = expert(n)
                                pe.wait_ge(xl_ready, n + 1)
                                for i, (bank, free, done) in enumerate(((bank_g[u], gs_ready, g_done),
                                                                        (bank_u[u], us_ready, u_done))):
                                    need(pe, free, n - 1)
                                    for k, (x, w) in enumerate(((XH, w_high), (XL, w_high), (XH, w_low))):
                                        mm = nc.tensor.matmul(bank[:, 0:W], x[:, r, :], w[:, i, e, :], start=(k == 0), stop=(k == 2))
                                    mm.then_inc(done, 1)
                            if exists(n, 2):
                                pe.wait_ge(xg_in[(r + 2) % 4], ring(n + 2, (r + 2) % 4))
                                need(pe, xl_ready, n + 2)
                                nc.tensor.transpose(bank_t[:, 0:P], XG[:, (r + 2) % 4, :], ident[:]).then_inc(t_done, 1)
                            if exists(n, -2):
                                e = held[(r + 2) % 4] if isinstance(n, int) or r >= 2 else expert(n - 2)
                                pe.wait_ge(ht_ready, n - 1)
                                need(pe, y_ready, n - 3)
                                for j in range(tiles):
                                    K = KD if j == 0 else F
                                    mm = nc.tensor.matmul(bank_y[u][:, 0:D], HT[0:K, u, j, :], dw[0:K, e, j, :],
                                                          start=(j == 0), stop=(j == tiles - 1))
                                mm.then_inc(y_done, 1)
                            if exists(n, -1):
                                pe.wait_ge(h_ready, n)
                                for j in range(tiles):
                                    mm = nc.tensor.transpose(bank_ht[0:F, P * j:P * j + P], H[:, v, F * j:F * j + F], ident[:])
                                mm.then_inc(ht_done, 1)

                        pipeline(pe, step)

                    @block.scalar
                    def _(act):
                        act.wait_ge(ones_done, 1)

                        def step(n, r):
                            u, v = r % 2, 1 - r % 2
                            if exists(n, 2):
                                act.wait_ge(t_done, n + 3)
                                need(act, u_done, n - 1)
                                nc.scalar.activation(XH[:, (r + 2) % 4, :], bank_t[:, 0:P], ACT.Copy).then_inc(xh_ready, 1)
                            if layer == 1 and exists(n, 0):
                                act.wait_ge(g_done, n + 1)
                                need(act, us_ready, n - 1)
                                nc.scalar.activation(GS[:, u, :], bank_g[u][:, 0:W], ACT.Silu).then_inc(gs_ready, 1)
                            if exists(n, -2):
                                act.wait_ge(y_done, n - 1)
                                if exists(n, -6):
                                    act.wait_ge(y_out[(r + 2) % 4], ring(n - 6, (r + 2) % 4))
                                nc.scalar.activation(Y[:, (r + 2) % 4, :], bank_y[u][:, 0:D], ACT.Copy).then_inc(y_ready, 1)
                            if exists(n, -1):
                                act.wait_ge(ht_done, n)
                                need(act, y_done, n - 2)
                                nc.scalar.activation(HT[0:F, v, :, :], bank_ht[0:F, 0:tiles * P].rearrange("p (j k) -> p j k", j=tiles),
                                                     ACT.Copy).then_inc(ht_ready, 1)
                            if layer == 0 and exists(n, 0):
                                act.wait_ge(hp_ready, n + 1)
                                need(act, ht_done, n - 1)
                                nc.scalar.activation(H[:, u, :], HP[:, u, :], ACT.Silu).then_inc(h_ready, 1)

                        pipeline(act, step)

                    @block.vector
                    def _(dve):
                        dve.wait_ge(params_read, 16 * N_PARAMS)

                        def low_part(n, r):
                            if exists(n, 2):
                                dve.wait_ge(xh_ready, n + 3)
                                need(dve, u_done, n - 1)
                                nc.vector.tensor_tensor(XL[:, (r + 2) % 4, :], bank_t[:, 0:P], XH[:, (r + 2) % 4, :].bitcast(F32),
                                                        ALU.subtract).then_inc(xl_ready, 1)

                        def step(n, r):
                            u, v = r % 2, 1 - r % 2
                            if layer == 1 or not exists(n, 0):
                                low_part(n, r)
                            if exists(n, 0) and layer == 0:
                                e = dve.value_load(expert_of[0:1, bass.ds(n, 1)], min_val=0, max_val=EXPERTS - 1)
                                dve.wait_ge(g_done, n + 1)
                                need(dve, hp_ready, n - 1)
                                nc.vector.tensor_tensor(GS[:, u, :], bank_g[u][:, 0:W], bias[:, 0, e, :], ALU.add).then_inc(gs_ready, 1)
                                dve.wait_ge(u_done, n + 1)
                                nc.vector.tensor_tensor(US[:, u, :], bank_u[u][:, 0:W], bias[:, 1, e, :], ALU.add).then_inc(us_ready, 1)
                                low_part(n, r)
                                dve.wait_ge(us_ready, n + 1)
                                need(dve, h_ready, n - 1)
                                nc.vector.tensor_tensor(HP[:, u, :], GS[:, u, :], US[:, u, :], ALU.mult).then_inc(hp_ready, 1)
                            if exists(n, 0) and layer == 1:
                                dve.wait_ge(u_done, n + 1)
                                dve.wait_ge(gs_ready, n + 1)
                                need(dve, ht_done, n - 1)
                                nc.vector.tensor_tensor(H[:, u, :], bank_u[u][:, 0:W], GS[:, u, :], ALU.mult).then_inc(us_ready, 1)

                        pipeline(dve, step)

        def combine(layer):
            QUARTER = B // 4
            last = layer == 1

            def quarter(i):
                return slice(QUARTER * i, QUARTER * i + QUARTER)

            with ExitStack() as inner:
                def sem(name):
                    return inner.enter_context(nc.semaphore(f"{name}_C{layer}"))

                R = inner.enter_context(nc.sbuf_tensor(f"R_C{layer}", [P, 2, B, D], F32))
                landed = [sem(f"landed{i}") for i in range(4)]
                scaled, first_done, x_done, stored = sem("scaled"), sem("first_done"), sem("x_done"), sem("stored")
                with nc.Block() as block:
                    @block.sync
                    def _(sp):
                        rows = results[0:TRASH].rearrange("(c b p) d -> p c b d", c=2, p=P)
                        for i in range(4):
                            for c in range(2):
                                sp.dma_start(R[:, c, quarter(i), :], rows[:, c, quarter(i), :]).then_inc(landed[i], 16)
                        if last:
                            for i in range(4):
                                sp.wait_ge(x_done, i + 1)
                                sp.dma_start(t["out"].rearrange("b p d -> p b d")[:, quarter(i), :],
                                             X[:, quarter(i), :]).then_inc(stored, 16)
                            sp.wait_ge(stored, 64)

                    @block.scalar
                    def _(act):
                        for i in range(4):
                            act.wait_ge(landed[i], 32)
                            for b in range(QUARTER * i, QUARTER * i + QUARTER):
                                ins = nc.scalar.activation(R[:, 1, b, :], R[:, 1, b, :], ACT.Copy, scale=weight[:, 1, b:b + 1])
                            ins.then_inc(scaled, 1)

                    @block.vector
                    def _(dve):
                        for i in range(4):
                            dve.wait_ge(landed[i], 32)
                            for b in range(QUARTER * i, QUARTER * i + QUARTER):
                                ins = nc.vector.scalar_tensor_tensor(X[:, b, :], R[:, 0, b, :], weight[:, 0, b:b + 1],
                                                                     X[:, b, :], ALU.mult, ALU.add)
                            ins.then_inc(first_done, 1)
                            dve.wait_ge(first_done, i + 1)
                            dve.wait_ge(scaled, i + 1)
                            nc.vector.tensor_tensor(X[:, quarter(i), :], X[:, quarter(i), :], R[:, 1, quarter(i), :],
                                                    ALU.add).then_inc(x_done, 1)

        def hidden(layer):
            width = t[f"L{layer}_gpT"].shape[2]
            tiles = -(-width // (P - 1)) if layer == 0 else width // P
            return tiles, width // tiles

        def clear_semaphores():
            used = sorted(nc.released_uncleared_semaphores)
            with nc.Block() as block:
                @block.gpsimd
                def _(pool):
                    first = used[0]
                    for number, following in zip(used, used[1:] + [None]):
                        if following != number + 1:
                            pool.sem_clear(range(first, number + 1))
                            first = following

        load_constants()
        for layer in range(2):
            with ExitStack() as held:
                tiles, F = hidden(layer)
                KD = F + 1 if layer == 0 else F

                def weights(name, shape, dtype=F32):
                    return held.enter_context(nc.sbuf_tensor(f"{name}_L{layer}", shape, dtype))

                gate, gate_b = weights("gate", [D, EXPERTS]), weights("gate_b", [P, EXPERTS])
                w_low, w_high = (weights(name, [D, 2, EXPERTS, tiles * F], F32R) for name in ("w_low", "w_high"))
                dw = weights("dw", [KD, EXPERTS, tiles, D])
                gate_in, gu_in, params_read, low_ready = (held.enter_context(nc.semaphore(f"{name}_L{layer}"))
                                                          for name in ("gate_in", "gu_in", "params_read", "low_ready"))
                attention(layer, prefetch=[(gate[:], t[f"L{layer}_gateT"], gate_in), (gate_b[:], t["L0_gateB"], gate_in),
                                        (w_low[:, 0, :, :].bitcast(F32), t[f"L{layer}_gpT"], gu_in),
                                        (w_low[:, 1, :, :].bitcast(F32), t[f"L{layer}_upT"], gu_in),
                                        (dw[:], t[f"L{layer}_downT"], params_read)])
                bias = weights("bias", [P, 2, EXPERTS, tiles * F]) if layer == 0 else None
                shared = (gate, gate_b, w_high, w_low, dw, bias, gate_in, gu_in, params_read, low_ready)
                route(layer, *shared)
                experts(layer, *shared)
            combine(layer)
            if layer == 0:
                clear_semaphores()


def _layouts(inputs):
    import numpy as np

    a = {k: np.asarray(v) for k, v in inputs.items()}
    out = {"x": a["x"], "ctx": a["ctx_1024"]}

    def heads_out(w):
        v = np.zeros((D, GROUPS, QUADS, SLOT), w.dtype)
        for part in range(3):
            v[..., HD * part:HD * part + HD] = w.T.reshape(D, GROUPS, QUADS, HD)
        return v.reshape(D, GROUPS, P)

    def heads_bias(b, one):
        v = np.zeros((QUADS, SLOT, GROUPS), b.dtype)
        for part in range(3):
            v[:, HD * part:HD * part + HD, :] = b.reshape(GROUPS, QUADS, HD).transpose(1, 2, 0)
        if one:
            v[:, ONES:ONES + 2, :] = 1
        return v.reshape(P, GROUPS)

    def low_rows(part):
        v = np.zeros((QUADS, SLOT, 1), np.float32)
        v[:, HD * part:HD * part + HD] = 1
        return v.reshape(P, 1)

    out["q_low"], out["k_low"] = low_rows(2), low_rows(1)
    for n in range(2):
        p = f"L{n}_xattn_"
        out[f"L{n}_WqP"] = heads_out(a[p + "Wq"])
        out[f"L{n}_WkP"] = heads_out(a[p + "Wk"])
        out[f"L{n}_WvT"] = a[p + "Wv"].T
        out[f"L{n}_WoT"] = a[p + "Wo"].T
        out[f"L{n}_bqP"] = heads_bias(a[p + "bq"], False)
        out[f"L{n}_bkP"] = heads_bias(a[p + "bk"], True)
        out[f"L{n}_bvB"] = np.broadcast_to(a[p + "bv"], (P, D))
        out[f"L{n}_boB"] = np.broadcast_to(a[p + "bo"], (P, D))
    out["L0_gateT"] = a["L0_ffn_gate_w"].T
    out["L1_gateT"] = a["L1_ffn_wg"].T
    out["L0_gateB"] = np.broadcast_to(a["L0_ffn_gate_b"], (P, EXPERTS))
    for n, g, u, dn, tiles in ((0, "L0_ffn_gp_w", "L0_ffn_up_w", "L0_ffn_down_w", 4),
                               (1, "L1_ffn_w1", "L1_ffn_w3", "L1_ffn_w2", 2)):
        F = a[g].shape[1] // tiles
        out[f"L{n}_gpT"] = a[g].transpose(2, 0, 1)
        out[f"L{n}_upT"] = a[u].transpose(2, 0, 1)
        dT = a[dn].transpose(2, 0, 1).reshape(tiles, F, EXPERTS, D).transpose(1, 2, 0, 3)
        if n == 0:
            full = np.zeros((F + 1, EXPERTS, tiles, D), dT.dtype)
            full[:F] = dT
            full[F, :, 0, :] = a["L0_ffn_down_b"]
            dT = full
        out[f"L{n}_downT"] = dT
    out["L0_biasB"] = np.broadcast_to(np.stack([a["L0_ffn_gp_b"], a["L0_ffn_up_b"]]), (P, 2, EXPERTS, a["L0_ffn_gp_b"].shape[1]))
    return {k: np.ascontiguousarray(v) for k, v in out.items()}


def kernel(**inputs):
    import numpy as _np
    import concourse.bacc as _bacc
    from concourse import mybir as _mybir
    from concourse.bass_utils import run_bass_kernel_spmd as _run

    nc = _bacc.Bacc("TRN2", target_bir_lowering=False, num_devices=1)
    arrays, tensors = {}, {}
    for name, a in _layouts(inputs).items():
        arrays[f"in_{name}"] = a
        tensors[name] = nc.dram_tensor(f"in_{name}", a.shape, _mybir.dt.from_np(a.dtype), kind="ExternalInput").ap()
    shape = inputs["x"].shape
    tensors["out"] = nc.dram_tensor("out_x", shape, F32, kind="ExternalOutput").ap()
    build_program(nc, tensors)
    r = _run(nc, [arrays], core_ids=[0])
    return r.results[0]["out_x"]
```
